# Optimizing a Trainium2 kernel written in Bass

```python
import numpy as np
import jax
import jax.numpy as jnp

def _softmax(x, axis=-1):
    return jax.nn.softmax(x, axis=axis)

def _gelu(x):
    return jax.nn.gelu(x, approximate=True)

def _silu(x):
    return jax.nn.silu(x)

def _sigmoid(x):
    return jax.nn.sigmoid(x)

def _layernorm(x, axis=-1, eps=1e-05):
    m = jnp.mean(x, axis=axis, keepdims=True)
    v = jnp.var(x, axis=axis, keepdims=True)
    return (x - m) / jnp.sqrt(v + eps)

def _scatter_add(tgt, idx, src, axis=0):
    return tgt.at[idx].add(src)

def _segment_sum(src, seg, n):
    return jax.ops.segment_sum(src, seg, n)
kernel_name = 'mk_vit_tower_d1_tok_img1024_r4_d0eb12'

def setup_inputs(seed: int=0):
    np.random.seed(seed)
    _w = jnp.asarray

    def _rec_inputs():
        import jax
        import jax.numpy as jnp
        _rk = jax.random.key(seed)
        x = jax.random.uniform(jax.random.fold_in(_rk, 1), (8, 3, 256, 256), jnp.float32, 0.0, 1)
        return x
    x = _rec_inputs()

    def _L0_tok_setup():
        import jax, jax.numpy as jnp
        import numpy as np
        _GRAY_W = (0.2989, 0.587, 0.114)
        key = jax.random.key(seed)
        x = jax.random.uniform(key, (32, 3, 256, 256), dtype=jnp.float32)
        sx = jnp.array([[-3.0, 0.0, 3.0], [-10.0, 0.0, 10.0], [-3.0, 0.0, 3.0]], dtype=jnp.float32)
        scharr = jnp.stack([sx, sx.T])[:, None, :, :]
        return {'x': x, 'scharr': scharr}
    _L0_tok_all = _L0_tok_setup()
    _L0_tok_in = {k: v for k, v in _L0_tok_all.items() if k in ('scharr',)}
    del _L0_tok_all

    def _L0_attn_setup():
        import jax, jax.numpy as jnp
        import numpy as np
        import math
        EMBED = 256
        HEADS = 16
        HEAD_DIM = EMBED // HEADS
        B, N = (2, 512)
        key = jax.random.key(seed)
        ks = jax.random.split(key, 8)
        s = 1.0 / math.sqrt(EMBED)
        Wq = jax.random.uniform(ks[0], (EMBED, EMBED), jnp.float32, -s, s)
        bq = jax.random.uniform(ks[1], (EMBED,), jnp.float32, -s, s)
        Wk = jax.random.uniform(ks[2], (EMBED, EMBED), jnp.float32, -s, s)
        bk = jax.random.uniform(ks[3], (EMBED,), jnp.float32, -s, s)
        Wv = jax.random.uniform(ks[4], (EMBED, EMBED), jnp.float32, -s, s)
        bv = jax.random.uniform(ks[5], (EMBED,), jnp.float32, -s, s)
        Wp = jax.random.normal(ks[6], (HEAD_DIM, HEAD_DIM), jnp.float32)
        x = jax.random.normal(ks[7], (B, N, EMBED), jnp.float32)
        return {'x': x, 'Wq': Wq, 'bq': bq, 'Wk': Wk, 'bk': bk, 'Wv': Wv, 'bv': bv, 'Wp': Wp}
    _L0_attn_all = _L0_attn_setup()
    _L0_attn_in = {k: v for k, v in _L0_attn_all.items() if k in ('Wq', 'bq', 'Wk', 'bk', 'Wv', 'bv', 'Wp')}
    del _L0_attn_all

    def _L0_ffn_setup():
        import jax, jax.numpy as jnp
        import numpy as np
        B, S, H, F, G = (8, 512, 256, 1024, 128)
        EPS = 1e-05

        def _dequant(q, scales, g):
            K, N = q.shape
            w = (q.astype(jnp.float32) - 128.0).reshape(K // g, g, N) * scales[:, None, :]
            return w.reshape(K, N)
        key = jax.random.key(seed)
        ks = jax.random.split(key, 8)
        x = jax.random.normal(ks[0], (B, S, H), dtype=jnp.float32)
        ln_gamma = jnp.ones((H,), jnp.float32)
        ln_beta = jnp.zeros((H,), jnp.float32)
        fc1_q = jax.random.randint(ks[1], (H, F), 0, 64, dtype=jnp.int32)
        fc2_q = jax.random.randint(ks[2], (F, H), 0, 64, dtype=jnp.int32)
        fc1_scales = jax.random.uniform(ks[3], (H // G, F), jnp.float32) * 0.02 + 0.001
        fc2_scales = jax.random.uniform(ks[4], (F // G, H), jnp.float32) * 0.02 + 0.001
        fc1_bias = jax.random.normal(ks[5], (F,), jnp.float32) * 0.02
        fc2_bias = jax.random.normal(ks[6], (H,), jnp.float32) * 0.02
        return {'x': x, 'ln_gamma': ln_gamma, 'ln_beta': ln_beta, 'fc1_q': fc1_q, 'fc1_scales': fc1_scales, 'fc1_bias': fc1_bias, 'fc2_q': fc2_q, 'fc2_scales': fc2_scales, 'fc2_bias': fc2_bias}
    _L0_ffn_all = _L0_ffn_setup()
    _L0_ffn_in = {k: v for k, v in _L0_ffn_all.items() if k in ('ln_gamma', 'ln_beta', 'fc1_q', 'fc1_scales', 'fc1_bias', 'fc2_q', 'fc2_scales', 'fc2_bias')}
    del _L0_ffn_all
    return {'x': x, 'L0_tok_scharr': _L0_tok_in['scharr'], 'L0_attn_Wq': _L0_attn_in['Wq'], 'L0_attn_bq': _L0_attn_in['bq'], 'L0_attn_Wk': _L0_attn_in['Wk'], 'L0_attn_bk': _L0_attn_in['bk'], 'L0_attn_Wv': _L0_attn_in['Wv'], 'L0_attn_bv': _L0_attn_in['bv'], 'L0_attn_Wp': _L0_attn_in['Wp'], 'L0_ffn_ln_gamma': _L0_ffn_in['ln_gamma'], 'L0_ffn_ln_beta': _L0_ffn_in['ln_beta'], 'L0_ffn_fc1_q': _L0_ffn_in['fc1_q'], 'L0_ffn_fc1_scales': _L0_ffn_in['fc1_scales'], 'L0_ffn_fc1_bias': _L0_ffn_in['fc1_bias'], 'L0_ffn_fc2_q': _L0_ffn_in['fc2_q'], 'L0_ffn_fc2_scales': _L0_ffn_in['fc2_scales'], 'L0_ffn_fc2_bias': _L0_ffn_in['fc2_bias']}

def reference(x, L0_tok_scharr, L0_attn_Wq, L0_attn_bq, L0_attn_Wk, L0_attn_bk, L0_attn_Wv, L0_attn_bv, L0_attn_Wp, L0_ffn_ln_gamma, L0_ffn_ln_beta, L0_ffn_fc1_q, L0_ffn_fc1_scales, L0_ffn_fc1_bias, L0_ffn_fc2_q, L0_ffn_fc2_scales, L0_ffn_fc2_bias):
    import jax
    import jax.numpy as jnp

    def _L0_tok_ref(x, scharr):
        import jax, jax.numpy as jnp
        import numpy as np
        _GRAY_W = (0.2989, 0.587, 0.114)
        w = jnp.asarray(_GRAY_W, dtype=x.dtype)
        gray = jnp.einsum('bchw,c->bhw', x, w)[:, None]
        edges = jax.lax.conv_general_dilated(gray, scharr, window_strides=(1, 1), padding='SAME', dimension_numbers=('NCHW', 'OIHW', 'NCHW'))
        abs_edges = jnp.sqrt(jnp.square(edges))
        edge = abs_edges.sum(axis=1) / 2
        return edge

    def _L0_attn_ref(x, Wq, bq, Wk, bk, Wv, bv, Wp):
        import jax, jax.numpy as jnp
        import numpy as np
        import math
        EMBED = 256
        HEADS = 16
        HEAD_DIM = EMBED // HEADS
        B, N = (2, 512)
        Bb, Nn, E = x.shape
        H, D = (HEADS, HEAD_DIM)
        q = (x @ Wq + bq).reshape(Bb, Nn, H, D)
        k = (x @ Wk + bk).reshape(Bb, Nn, H, D)
        v = (x @ Wv + bv).reshape(Bb, Nn, H, D)
        q = jnp.einsum('bnhe,ei->bnhi', q, Wp)
        k = jnp.einsum('bnhe,ei->bnhi', k, Wp)
        scores = jnp.einsum('bnhi,bmhi->bnhm', q, k) / math.sqrt(D)
        attn = jax.nn.softmax(scores, axis=-1)
        out = jnp.einsum('bnhm,bmhe->bnhe', attn, v).reshape(Bb, Nn, E)
        return out

    def _L0_ffn_ref(x, ln_gamma, ln_beta, fc1_q, fc1_scales, fc1_bias, fc2_q, fc2_scales, fc2_bias):
        import jax, jax.numpy as jnp
        import numpy as np
        B, S, H, F, G = (8, 512, 256, 1024, 128)
        EPS = 1e-05

        def _dequant(q, scales, g):
            K, N = q.shape
            w = (q.astype(jnp.float32) - 128.0).reshape(K // g, g, N) * scales[:, None, :]
            return w.reshape(K, N)
        residual = x
        mu = jnp.mean(x, axis=-1, keepdims=True)
        var = jnp.mean(jnp.square(x - mu), axis=-1, keepdims=True)
        h = (x - mu) * jax.lax.rsqrt(var + EPS) * ln_gamma + ln_beta
        hf = h.reshape(-1, H)
        w1 = _dequant(fc1_q, fc1_scales, G)
        y = hf @ w1 + fc1_bias
        y = jax.nn.silu(y)
        w2 = _dequant(fc2_q, fc2_scales, G)
        z = y @ w2 + fc2_bias
        return residual + 0.5 * z.reshape(residual.shape)
    h = _L0_tok_ref(x, L0_tok_scharr)
    h = h + _L0_attn_ref(_layernorm(h, axis=-1), L0_attn_Wq, L0_attn_bq, L0_attn_Wk, L0_attn_bk, L0_attn_Wv, L0_attn_bv, L0_attn_Wp)
    h = h + _L0_ffn_ref(_layernorm(h, axis=-1), L0_ffn_ln_gamma, L0_ffn_ln_beta, L0_ffn_fc1_q, L0_ffn_fc1_scales, L0_ffn_fc1_bias, L0_ffn_fc2_q, L0_ffn_fc2_scales, L0_ffn_fc2_bias)
    return h

_drawn_inputs = setup_inputs


def setup_inputs(seed=0):
    import zlib

    import numpy as np

    out = dict(_drawn_inputs(seed))
    spreads = {'L0_ffn_ln_gamma': (1.0, 0.2), 'L0_ffn_ln_beta': (0.0, 0.1)}
    factors = {}
    for name, (base, spread) in spreads.items():
        noise = np.random.default_rng([zlib.crc32(name.encode()), seed]).standard_normal(out[name].shape)
        drawn = base * np.exp(spread * noise) if base else spread * noise
        out[name] = jnp.asarray(drawn.astype(out[name].dtype))
    for name, factor in factors.items():
        out[name] = (out[name] * factor).astype(out[name].dtype)
    return out
```

```python
import concourse.bass as bass
from concourse import mybir
from contextlib import ExitStack


def vit_tower_kernel(nc, x, scharr, Wq, bq, Wk, bk, Wv, bv, Wp, ln_gamma, ln_beta,
                     fc1_q, fc1_scales, fc1_bias, fc2_q, fc2_scales, fc2_bias, out):
    fp32 = mybir.dt.float32
    fp32r = mybir.dt.float32r
    i32 = mybir.dt.int32
    ALU = mybir.AluOpType
    ACT = mybir.ActivationFunctionType
    AX = mybir.AxisListType

    P = 128
    B, C, N, E = x.shape
    NT = N // P
    KE = E // P
    D = Wp.shape[0]
    HEADS = E // D
    HPT = P // D
    F = fc1_q.shape[1]
    FT = F // P
    PAIRS = B // 2
    COLS = 2 * N
    EPS = 1e-5
    GRAY = (0.2989, 0.587, 0.114)
    Q_SCALE = float(D) ** -0.5
    SPLIT = 3 * D
    MROW = 96
    KSTACK = MROW + 2
    VW = D + 1
    OROWS = 32

    KB = 1024
    base = (nc.sbuf_base + 63) // 64 * 64

    def at(name, kb, shape, dt):
        size = 4
        for n in shape[1:]:
            size *= n
        assert base + int(kb * KB) + size <= nc.sbuf_usable_end, name
        return nc.alloc_sbuf_tensor_at(name, shape, dt, offset=base + int(kb * KB))

    hid = at("hid", 0, [P, PAIRS, NT, 2, E], fp32)
    ident = at("ident", 16, [P, P], fp32)
    stats = at("stats", 16.5, [P, 4, 6], fp32)
    mv = at("mv", 16.625, [P, 4, 2], fp32)
    rstd = at("rstd", 16.75, [P, 4], fp32)
    mhalf = at("mhalf", 16.8125, [P, 4], fp32)
    vareps = at("vareps", 16.875, [P, 4], fp32)
    stats3 = at("stats3", 17, [P, 4, 6], fp32)
    mv3 = at("mv3", 17.125, [P, 4, 2], fp32)
    rstd3 = at("rstd3", 17.25, [P, 4], fp32)
    vareps3 = at("vareps3", 17.3125, [P, 4], fp32)
    negmax = at("negmax", 17.375, [P, NT, HEADS], fp32)
    qk_bias = at("qk_bias", 17.5, [P, 2, KE], fp32)
    qk_bcol = at("qk_bcol", 17.5625, [P, 2, KE], fp32)
    recip = at("recip", 24.75, [P, 2, HEADS], fp32)
    gamma = at("gamma", 17.6875, [P, KE], fp32)
    beta = at("beta", 17.75, [P, KE], fp32)
    b1col = at("b1col", 17.8125, [P, FT], fp32)
    b1 = at("b1", 17.875, [P, FT], fp32)
    halo_m = at("halo_m", 17.9375, [P, NT, 3], fp32)
    halo_p = at("halo_p", 18, [P, NT, 2, 3], fp32)
    halo_w = at("halo_w", 18.0625, [P, NT * 2], fp32)
    halo_wh = at("halo_wh", 18.125, [P, NT * 2], fp32r)
    halo_wl = at("halo_wl", 18.1875, [P, NT * 2], fp32)
    s_all = at("s_all", 18.25, [P, 18], fp32)
    onecol = at("onecol", 18.375, [P, 1], fp32)
    negsplit = at("negsplit", 18.5, [P, NT, 2, 8], fp32)
    negrow = at("negrow", 18.75, [16, 2, N], fp32r)
    b2 = at("b2", 20.75, [P, 4, E], fp32)

    xr = at("xr", 25, [P, 2, C, NT, E], fp32)
    gray = at("gray", 37, [P, 2, NT, E], fp32)
    gray_h = at("gray_h", 41, [P, NT, 2, E + 2], fp32r)
    gray_l = at("gray_l", 45.25, [P, NT, 2, E + 2], fp32r)
    band_h = at("band_h", 49.5, [P, 2, 3, P], fp32r)
    band_l = at("band_l", 52.5, [P, 2, 3, P], fp32r)
    halo = at("halo", 55.5, [P, B, E], fp32r)
    halo_b = at("halo_b", 63.5, [P, NT, 2, P], fp32r)
    w1_h = at("w1_h", 25, [P, KE, F], fp32r)
    w1_l = at("w1_l", 33, [P, KE, F], fp32r)
    wraw = at("wraw", 41, [P, KE * F], i32)
    wscale = at("wscale", 49, [P, KE * F], fp32)
    wfull = at("wfull", 57, [P, KE * F], fp32)

    xn = at("xn", 66, [P, NT, 2, E], fp32)
    xt_h = at("xt_h", 70, [P, KE, COLS], fp32r)
    xt_l = at("xt_l", 74, [P, KE, COLS], fp32r)
    qk_h = at("qk_h", 78, [P, 2, COLS], fp32r)
    qk_l = at("qk_l", 82, [P, 2, COLS], fp32r)
    wqk_h = at("wqk_h", 86, [P, KE, 3 * E], fp32r)
    wqk_l = at("wqk_l", 92, [P, KE, 3 * E], fp32r)
    bv2 = at("bv2", 98, [P, NT, E], fp32)
    vals = at("vals", 100, [P, 4, NT, HEADS * VW + 16], fp32)
    otr = at("otr", 109.25, [P, 4, N], fp32)
    absd = at("absd", 113.25, [P, COLS], fp32)
    att = at("att", 115.25, [P, 2, E], fp32)
    probs = at("probs", 117.25, [P, 8, NT * N], fp32)
    qs = at("qs", 133.25, [P, 2, HEADS, N], fp32r)
    ks = at("ks", 165.25, [P, 2, HEADS, N], fp32r)
    assert 197.25 + 8 <= (nc.sbuf_usable_end - base) / KB
    zeros = at("zeros", 205.25, [P, E], fp32)
    masks = at("masks", 117.25, [P, 3, P], fp32)
    band = at("band", 119, [P, 2, 3, P], fp32)
    halo_x = at("halo_x", 122.25, [32, B, E], fp32)
    wsrc = at("wsrc", 197.25, [P, 2, KE, E], fp32)
    wtr = at("wtr", 201.25, [P, 2, KE * E], fp32)
    wv_src = at("wv_src", 109.25, [P, KE, E], fp32)
    wp_diag = at("wp_diag", 111.25, [P, P], fp32)
    wp_rep = at("wp_rep", 111.75, [P, D], fp32)

    w2_h = at("w2_h", 66, [P, FT, E], fp32r)
    w2_l = at("w2_l", 74, [P, FT, E], fp32r)
    nt_h = at("nt_h", 82, [P, KE, COLS], fp32r)
    nt_l = at("nt_l", 86, [P, KE, COLS], fp32r)
    xp = at("xp", 90, [P, NT, 2, E], fp32)
    n3 = at("n3", 94, [P, NT, 2, E], fp32)
    res = at("res", 98, [P, 2, 4, E], fp32)
    yf = at("yf", 106, [P, 2, COLS], fp32)
    osb = at("osb", 110, [P, 2, COLS], fp32)
    y_h = at("y_h", 133.25, [P, 2, FT, COLS], fp32r)
    y_l = at("y_l", 165.25, [P, 2, FT, COLS], fp32r)

    qk_dram = nc.dram_tensor("qk_parts", [PAIRS, 2, 2, E, COLS], fp32).ap()
    neg_dram = nc.dram_tensor("neg_parts", [B, 2, 16, N], fp32).ap()

    ctx = ExitStack()
    with ctx:
        def bank(name):
            return ctx.enter_context(nc.psum_tensor(name, [P, COLS], fp32))

        def sem(name):
            return ctx.enter_context(nc.semaphore(name))

        p1 = [bank("p1a"), bank("p1b"), bank("p1c")]
        p2 = [bank("p2a"), bank("p2b")]
        av = bank("av")
        mi = [bank("mia"), bank("mib")]

        s_scharr = sem("scharr_loaded")
        s_cleared = sem("cleared")
        s_halo = sem("halo_loaded")
        s_wld = sem("attn_weights_loaded")
        s_wpd = sem("wp_loaded")
        s_x = [sem("x_loaded0"), sem("x_loaded1")]
        s_wraw = sem("ffn_weights_loaded")
        s_small = sem("small_loaded")
        s_masks = sem("masks_ready")
        s_zero = sem("zeroed")
        s_zeros = sem("zeros_ready")
        s_border = sem("gray_borders_zeroed")
        s_ones = sem("stacks_preset")
        s_band = sem("band_ready")
        s_halo_h = sem("halo_high_ready")
        s_halo_w = sem("halo_operands_ready")
        s_wt = sem("w_transposed")
        s_wtc = sem("w_transpose_copied")
        s_fold = sem("w_folded")
        s_wready = sem("qkv_weights_ready")
        s_dv = sem("vector_chain")
        s_pl = sem("pool_chain")
        s_gray = sem("gray_split")
        s_grayp = sem("gray_ready")
        s_grayh = sem("gray_high_ready")
        s_edges = sem("edges_added")
        s_mv = sem("moments_ready")
        s_rstd = sem("rstd_ready")
        s_xn = sem("xn_ready")
        s_fill = [sem("misc_filled0"), sem("misc_filled1")]
        s_free = [sem("misc_freed0"), sem("misc_freed1")]
        s_hi = sem("high_part_ready")
        s_store = [sem("qk_stored0"), sem("qk_stored1")]
        s_load = [[sem(f"qk_loaded{b}{h}") for h in range(2)] for b in range(2)]
        s_p1 = sem("p1_scores")
        s_max = sem("maxima")
        s_split = sem("neg_max_split")
        s_nst = sem("neg_rows_stored")
        s_nld = [sem("neg_rows_loaded0"), sem("neg_rows_loaded1")]
        s_p2 = sem("p2_scores")
        s_exp = sem("exps")
        s_av = sem("av_groups")
        s_ot = sem("av_copied")
        s_h2 = sem("attention_added")
        s_w1f = sem("w_full")
        s_w1r = sem("w1_ready")
        s_w2r = sem("w2_ready")
        s_mv2 = sem("moments2")
        s_rs2 = sem("rstd2")
        s_xp = sem("xp_ready")
        s_mv3 = sem("moments3")
        s_rs3 = sem("rstd3_ready")
        s_n3 = sem("n3_ready")
        s_res = sem("residual_ready")
        s_f1 = sem("fc1_done")
        s_silu = sem("silu_done")
        s_y = sem("y_ready")
        s_f2 = sem("fc2_done")
        s_osb = sem("out_rows_ready")
        s_out = [sem("out_stored0"), sem("out_stored1")]

        turns = []

        def tok_turns(p):
            turns.extend(("tok", p, i) for i in range(2 * NT))

        def xt_turns(p):
            turns.extend(("xt", p, i) for i in range(KE))

        def qkv_turns(p):
            turns.extend(("qkv", p, i) for i in range(6))

        QKV = [(0, 0), (1, 0), None, (0, 1), (1, 1), None]
        tok_turns(0)
        xt_turns(0)
        qkv_turns(0)
        tok_turns(1)
        AT_AV_LAST, AT_NEG1, AT_OUT, AT_XT, AT_QKV, AT_TOK, AT_NEG0 = 1, 2, 3, 4, (5, 6, 7, 8, 9, 10), (4, 6, 8, 10), 9
        AT_AV = (5, 9, 13)
        AT_B1, AT_N3 = 12, 12

        def has_xt(s):
            return s % 2 == 1 and (s + 1) // 2 < PAIRS

        def has_tok(s):
            return s % 2 == 0 and s >= 2 and s // 2 + 1 < PAIRS

        for s in range(B + 2):
            for i in range(HEADS):
                if i == AT_NEG1 and 1 <= s <= B:
                    turns.append(("neg", s - 1, 1))
                if i == AT_OUT and s >= 2:
                    turns.extend(("out", s - 2, t) for t in range(NT))
                if has_xt(s) and i == AT_XT:
                    xt_turns((s + 1) // 2)
                if has_xt(s) and i in AT_QKV:
                    turns.append(("qkv", (s + 1) // 2, AT_QKV.index(i)))
                if has_tok(s) and i in AT_TOK:
                    turns.append(("tok", s // 2 + 1, AT_TOK.index(i)))
                if i == AT_NEG0 and s < B:
                    turns.append(("neg", s, 0))
                if s == B - 1 and i == AT_B1:
                    turns.append(("b1", 0, 0))
                if s == B and i == AT_N3:
                    turns.extend(("n3", 0, kf) for kf in range(KE))
        for p in range(1, PAIRS):
            turns.extend(("n3", p, kf) for kf in range(KE))
        turn = {key: n for n, key in enumerate(turns)}
        assert len(turn) == len(turns)

        def misc(key):
            return mi[turn[key] % 2]

        def wait_filled(eng, key):
            n = turn[key]
            eng.wait_ge(s_fill[n % 2], n // 2 + 1)

        def wait_freed(eng, key):
            n = turn[key]
            if n >= 2:
                eng.wait_ge(s_free[n % 2], n // 2)

        def wait_read(eng, key):
            n = turn[key]
            eng.wait_ge(s_free[n % 2], n // 2 + 1)

        def filled(key):
            return s_fill[turn[key] % 2]

        def freed(key):
            return s_free[turn[key] % 2]

        block = ctx.enter_context(nc.Block())

        @block.sync
        def _(eng):
            def load_x(b):
                if b >= 2:
                    eng.wait_ge(s_grayp, b - 1)
                eng.dma_start(xr[:, b % 2], x[b].rearrange("c (t p) w -> p c t w", p=P)).then_inc(s_x[b % 2], 16)

            def store_qk(p, i):
                n = 4 * p + i
                op, m = (i % 2, i // 2)
                wait_read(eng, ("qkv", p, i + i // 2))
                for part, src in enumerate((qk_h, qk_l)):
                    eng.dma_start(qk_dram[p, op, part, m * P:(m + 1) * P, :], src[:, n % 2, :].bitcast(fp32)).then_inc(s_store[n % 2], 16)

            def load_qk(b, half):
                p = b // 2
                for r in range(2):
                    eng.wait_ge(s_store[r], 32 * (2 * p + half + 1))
                if b >= 2:
                    eng.wait_ge(s_p2, HEADS * (b - 2) + 8 * (half + 1))
                else:
                    eng.wait_ge(s_ones, 4)
                cols = slice((b % 2) * N, (b % 2 + 1) * N)
                for dst, op, parts in ((qs, 0, (0, 1, 0)), (ks, 1, (0, 0, 1))):
                    for slot, part in enumerate(parts):
                        src = qk_dram[p, op, part, half * P:(half + 1) * P, cols].rearrange("(h d) t -> d h t", d=D)
                        eng.dma_start(dst[slot * D:(slot + 1) * D, b % 2, half * HPT:(half + 1) * HPT, :].bitcast(fp32), src)\
                           .then_inc(s_load[b % 2][half], 16)

            def pass_neg(b, half):
                u = 2 * b + half
                wait_read(eng, ("neg", b, half))
                eng.dma_start(neg_dram[b, half], negrow[:, u % 2, :].bitcast(fp32)).then_inc(s_nst, 16)
                eng.wait_ge(s_nst, 16 * (u + 1))
                if b >= 2:
                    eng.wait_ge(s_p2, HEADS * (b - 2) + 8 * (half + 1))
                eng.dma_start(qs[MROW:MROW + 2, b % 2, half * HPT:(half + 1) * HPT, :].bitcast(fp32),
                              neg_dram[b, half].rearrange("(r h) t -> r h t", r=2)).then_inc(s_nld[half], 16)

            eng.dma_start(s_all[:], scharr.rearrange("k o a b -> o (k a b)").broadcast_to([P, 18])).then_inc(s_scharr, 16)
            load_x(0)
            eng.dma_start(wsrc[:, 0], Wq.rearrange("(k p) n -> p k n", p=P)).then_inc(s_wld, 16)
            eng.dma_start(wsrc[:, 1], Wk.rearrange("(k p) n -> p k n", p=P)).then_inc(s_wld, 16)
            eng.dma_start(wp_rep[:], Wp.unsqueeze(0).broadcast_to([HPT, D, D])).then_inc(s_wpd, 16)
            load_x(1)
            for i, src in enumerate((bq, bk)):
                eng.dma_start(qk_bcol[:, i, :], src.rearrange("(m p) -> p m", p=P), allow_slow_non_contiguous=True).then_inc(s_wpd, 16)
            eng.dma_start(wv_src[:], Wv.rearrange("(k p) n -> p k n", p=P)).then_inc(s_wld, 16)
            for t in range(NT):
                eng.dma_start(bv2[:, t, :], bv.rearrange("(a n) -> a n", a=1).broadcast_to([P, E])).then_inc(s_wld, 16)
            load_x(2)
            load_x(3)
            for dst, src in ((gamma, ln_gamma), (beta, ln_beta), (b1col, fc1_bias)):
                eng.dma_start(dst[:], src.rearrange("(m p) -> p m", p=P), allow_slow_non_contiguous=True).then_inc(s_small, 16)
            for j in range(4):
                eng.dma_start(b2[:, j, :], fc2_bias.rearrange("(a n) -> a n", a=1).broadcast_to([P, E])).then_inc(s_small, 16)
            for i in range(4):
                store_qk(0, i)
            for half in range(2):
                load_qk(0, half)
            for half in range(2):
                load_qk(1, half)
            load_x(4)
            load_x(5)
            for s in range(B + 1):
                if s >= 1:
                    pass_neg(s - 1, 1)
                if s == 2:
                    load_x(6)
                    load_x(7)
                if has_xt(s):
                    store_qk((s + 1) // 2, 0)
                    store_qk((s + 1) // 2, 1)
                if 1 <= s and s + 1 < B:
                    load_qk(s + 1, 0)
                if has_xt(s):
                    store_qk((s + 1) // 2, 2)
                if s < B:
                    pass_neg(s, 0)
                if has_xt(s):
                    store_qk((s + 1) // 2, 3)
                if 1 <= s and s + 1 < B:
                    load_qk(s + 1, 1)
                if s == 5:
                    wait_filled(eng, ("tok", PAIRS - 1, 2 * NT - 1))
                    eng.dma_start(wraw[:].rearrange("p (k n) -> p k n", k=KE), fc1_q.rearrange("(k p) n -> p k n", p=P)).then_inc(s_wraw, 16)
                    eng.dma_start(wscale[:], fc1_scales.rearrange("(a g) n -> a (g n)", a=1).broadcast_to([P, KE * F])).then_inc(s_wraw, 16)
                if s == 7:
                    eng.wait_ge(s_w1f, 1)
                    eng.dma_start(wraw[:].rearrange("p (k n) -> p k n", k=FT), fc2_q.rearrange("(k p) n -> p k n", p=P)).then_inc(s_wraw, 16)
                    eng.dma_start(wscale[:], fc2_scales.rearrange("(a g) n -> a (g n)", a=1).broadcast_to([P, FT * E])).then_inc(s_wraw, 16)
            for p in range(PAIRS):
                for h in range(2):
                    u = 2 * p + h
                    eng.wait_ge(s_osb, u + 1)
                    for b in range(2):
                        dst = out[2 * p + b, h * P:(h + 1) * P, :]
                        eng.dma_start(dst, osb[:, u % 2, b * E:(b + 1) * E]).then_inc(s_out[u % 2], 16)
            for r in range(2):
                eng.wait_ge(s_out[r], 32 * PAIRS)

        @block.gpsimd
        def _(eng):
            chain = [0]

            def link(ins):
                chain[0] += 1
                ins.then_inc(s_pl, 1)
                eng.wait_ge(s_pl, chain[0])

            eng.memset(halo_x[:], 0.0).then_inc(s_cleared, 1)
            link(eng.memset(onecol[:], 0.0))
            eng.memset(zeros[:], 0.0).then_inc(s_zeros, 1)
            eng.wait_ge(s_zeros, 1)
            eng.memset(onecol[MROW:P], 1.0).then_inc(s_zeros, 1)
            eng.wait_ge(s_zeros, 2)
            link(eng.memset(masks[:], 0.0))
            for r in range(3):
                ins = eng.affine_select(out=masks[:, r], in_=masks[:, r], compare_op=ALU.not_equal, fill=1.0,
                                        base=1 - r, pattern=[[-1, P]], channel_multiplier=1)
                ins.then_inc(s_masks, 1)
            eng.memset(ident[:], 0.0).then_inc(s_zero, 1)
            eng.wait_ge(s_zero, 1)
            eng.affine_select(out=ident[:], in_=ident[:], compare_op=ALU.not_equal, fill=1.0,
                              base=0, pattern=[[-1, P]], channel_multiplier=1).then_inc(s_masks, 1)
            link(eng.memset(halo_m[:], 0.0))
            for q in (0, 32, 64):
                for c in range(C):
                    rows = halo_m[q:q + 32]
                    link(eng.affine_select(out=rows, in_=rows, compare_op=ALU.not_equal, fill=GRAY[c],
                                           base=-6 * c, pattern=[[-3, NT], [-1, 3]], channel_multiplier=1))
            eng.memset(halo[96:128].bitcast(fp32), 0.0).then_inc(s_zero, 1)
            eng.wait_ge(s_zero, 2)
            eng.wait_ge(s_wpd, 48)
            diag = wp_diag[:].rearrange("p (h e) -> p h e", e=D)
            link(eng.affine_select(out=diag, in_=wp_rep[:].unsqueeze(1).broadcast_to([P, HPT, D]), compare_op=ALU.is_ge, fill=0.0,
                                   base=0, pattern=[[-D, HPT], [0, D]], channel_multiplier=1))
            eng.affine_select(out=diag, in_=diag, compare_op=ALU.is_ge, fill=0.0,
                              base=D - 1, pattern=[[D, HPT], [0, D]], channel_multiplier=-1).then_inc(s_masks, 1)
            eng.wait_ge(s_masks, 5)
            eng.memset(mhalf[:], -0.5).then_inc(s_zero, 1)
            eng.wait_ge(s_wready, 5)
            eng.memset(vals[:], 1.0).then_inc(s_zero, 1)
            for b in range(2):
                eng.memset(qs[:, b].bitcast(fp32), 0.0).then_inc(s_ones, 1)

            def rstd_of(mv_t, ve, dst, ready, n, done):
                eng.wait_ge(ready, n)
                link(eng.tensor_scalar(ve[:], mv_t[:, :, 1], EPS, 1.0, ALU.add, ALU.mult))
                eng.tensor_tensor(dst[:], ve[:], mhalf[:], ALU.pow).then_inc(done, 1)

            def gray_image(b):
                p = b // 2
                eng.wait_ge(s_x[b % 2], 16 * (b // 2 + 1))
                g = gray[:, b % 2]
                if b >= 2:
                    eng.wait_ge(s_gray, b - 1)
                ch = [xr[:, b % 2, c] for c in range(C)]
                link(eng.tensor_scalar(g, ch[0], GRAY[0], 0.0, ALU.mult, ALU.add))
                for c in range(1, C):
                    link(eng.tensor_scalar(ch[c], ch[c], GRAY[c], 0.0, ALU.mult, ALU.add))
                    ins = eng.tensor_tensor(g, g, ch[c], ALU.add)
                    if c < C - 1:
                        link(ins)
                ins.then_inc(s_grayp, 1)
                eng.wait_ge(s_grayp, b + 1)
                if p >= 1:
                    wait_filled(eng, ("tok", p - 1, 2 * NT - 1))
                eng.tensor_scalar(gray_h[:, :, b % 2, 1:E + 1], g, 1.0, 0.0, ALU.mult, ALU.add).then_inc(s_grayh, 1)

            def add_attention(b):
                for t in range(NT):
                    u = NT * b + t
                    wait_read(eng, ("out", b, t))
                    h = hid[:, b // 2, t, b % 2, :]
                    eng.tensor_tensor(h, h, att[:, u % 2, :], ALU.add).then_inc(s_h2, 1)

            rstd_of(mv, vareps, rstd, s_mv, 1, s_rstd)
            gray_image(2)
            gray_image(3)
            rstd_of(mv, vareps, rstd, s_mv, 2, s_rstd)
            for s in range(1, B + 2):
                if s >= 2:
                    add_attention(s - 2)
                if s in (1, 3):
                    gray_image(s + 3)
                    gray_image(s + 4)
                if s in (2, 4):
                    rstd_of(mv, vareps, rstd, s_mv, s // 2 + 2, s_rstd)
                if s == 6:
                    eng.wait_ge(s_wraw, 32)
                    link(eng.tensor_scalar(wfull[:], wraw[:], -128.0, 1.0, ALU.add, ALU.mult))
                    eng.tensor_tensor(wfull[:], wfull[:], wscale[:], ALU.mult).then_inc(s_w1f, 1)
                if s == 8:
                    rstd_of(mv, vareps, rstd, s_mv2, 1, s_rs2)
                    rstd_of(mv3, vareps3, rstd3, s_mv3, 1, s_rs3)
                    eng.wait_ge(s_wraw, 64)
                    eng.wait_ge(s_w1r, 2)
                    wait_filled(eng, ("b1", 0, 0))
                    link(eng.tensor_scalar(wfull[:], wraw[:], -128.0, 0.5, ALU.add, ALU.mult))
                    eng.tensor_tensor(wfull[:], wfull[:], wscale[:], ALU.mult).then_inc(s_w1f, 1)
            eng.wait_ge(s_small, 16 * 7)
            link(eng.tensor_scalar(b2[:], b2[:], 0.5, 0.0, ALU.mult, ALU.add))
            for p in range(PAIRS):
                if p >= 1:
                    rstd_of(mv, vareps, rstd, s_mv2, p + 1, s_rs2)
                    rstd_of(mv3, vareps3, rstd3, s_mv3, p + 1, s_rs3)
                eng.wait_ge(s_xp, p + 1)
                if p >= 2:
                    eng.wait_ge(s_osb, 2 * (p - 1))
                r = res[:, p % 2].rearrange("p j e -> p (j e)")
                link(eng.tensor_tensor(r, hid[:, p].rearrange("p t b e -> p (t b e)"), xp[:].rearrange("p t b e -> p (t b e)"), ALU.add))
                eng.tensor_tensor(r, r, b2[:].rearrange("p j e -> p (j e)"), ALU.add).then_inc(s_res, 1)

        @block.vector
        def _(eng):
            chain = [0]

            def link(ins):
                chain[0] += 1
                ins.then_inc(s_dv, 1)
                eng.wait_ge(s_dv, chain[0])

            for g in (gray_h, gray_l):
                for c in (0, E + 1):
                    eng.memset(g[:, :, :, c:c + 1].bitcast(fp32), 0.0).then_inc(s_border, 1)
            eng.wait_ge(s_scharr, 16)
            eng.wait_ge(s_masks, 4)
            for k in range(2):
                for dx in range(3):
                    for dy in range(3):
                        w = s_all[:, 9 * k + 3 * dy + dx:9 * k + 3 * dy + dx + 1]
                        if dy == 0:
                            link(eng.tensor_scalar(band[:, k, dx], masks[:, dy], w, None, ALU.mult))
                        else:
                            link(eng.scalar_tensor_tensor(out=band[:, k, dx], in0=masks[:, dy], scalar=w,
                                                          in1=band[:, k, dx], op0=ALU.mult, op1=ALU.add))
            link(eng.tensor_scalar(band_h[:], band[:], 0.5, None, ALU.mult))
            eng.scalar_tensor_tensor(out=band_l[:].rearrange("p k d j -> p (k d j)"), in0=band[:].rearrange("p k d j -> p (k d j)"),
                                     scalar=0.5, in1=band_h[:].rearrange("p k d j -> p (k d j)").bitcast(fp32),
                                     op0=ALU.mult, op1=ALU.subtract).then_inc(s_band, 1)

            def gray_first(b):
                eng.wait_ge(s_x[b % 2], 16)
                g = gray[:, b % 2]
                link(eng.tensor_scalar(g, xr[:, b % 2, 0], GRAY[0], None, ALU.mult))
                link(eng.scalar_tensor_tensor(out=g, in0=xr[:, b % 2, 1], scalar=GRAY[1], in1=g, op0=ALU.mult, op1=ALU.add))
                eng.scalar_tensor_tensor(out=g, in0=xr[:, b % 2, 2], scalar=GRAY[2], in1=g, op0=ALU.mult, op1=ALU.add).then_inc(s_grayp, 1)
                eng.wait_ge(s_grayp, b + 1)
                eng.tensor_scalar(gray_h[:, :, b % 2, 1:E + 1], g, 1.0, None, ALU.mult).then_inc(s_grayh, 1)

            def gray_low(b):
                eng.wait_ge(s_grayh, b + 1)
                eng.tensor_tensor(gray_l[:, :, b % 2, 1:E + 1], gray[:, b % 2], gray_h[:, :, b % 2, 1:E + 1].bitcast(fp32),
                                  ALU.subtract).then_inc(s_gray, 1)

            gray_first(0)
            gray_low(0)
            gray_first(1)
            gray_low(1)
            eng.wait_ge(s_zero, 2)
            for t in range(NT):
                dy = 2 if t == 0 else 0
                ins = eng.tensor_tensor(halo_p[:, t], halo_m[:, t].unsqueeze(1).broadcast_to([P, 2, 3]),
                                        s_all[:].rearrange("p (k a) -> p k a", k=2)[:, :, 3 * dy:3 * dy + 3], ALU.mult)
            link(ins)
            link(eng.tensor_reduce(halo_w[:], halo_p[:].rearrange("p t k x -> p (t k) x"), AX.X, ALU.add))
            link(eng.tensor_scalar(halo_wh[:], halo_w[:], 0.5, None, ALU.mult))
            link(eng.scalar_tensor_tensor(out=halo_wl[:], in0=halo_w[:], scalar=0.5, in1=halo_wh[:].bitcast(fp32),
                                          op0=ALU.mult, op1=ALU.subtract))
            eng.wait_ge(s_halo_h, 2)
            eng.tensor_tensor(halo[64:96], halo_x[:], halo[0:32].bitcast(fp32), ALU.subtract).then_inc(s_halo_w, 1)
            link(eng.memset(halo_b[:].bitcast(fp32), 0.0))
            for t in range(NT):
                edge = P - 1 if t == 0 else 0
                link(eng.tensor_copy(halo_b[:, t, :, edge], halo_wh[:, 2 * t:2 * t + 2].bitcast(fp32)))
                ins = eng.tensor_copy(halo_b[32:64, t, :, edge], halo_wl[32:64, 2 * t:2 * t + 2])
                if t == 0:
                    link(ins)
            ins.then_inc(s_halo_w, 1)

            eng.wait_ge(s_wld, 16 * 5)
            link(eng.tensor_copy(wqk_h[:, :, 2 * E:], wv_src[:]))
            eng.tensor_tensor(wqk_l[:, :, 2 * E:], wv_src[:], wqk_h[:, :, 2 * E:].bitcast(fp32), ALU.subtract).then_inc(s_wready, 1)
            for op in range(2):
                scale = Q_SCALE if op == 0 else 1.0
                eng.wait_ge(s_fold, op + 1)
                folded = p1[op][:, :].rearrange("p (k n) -> p k n", k=KE)
                cols = slice(op * E, (op + 1) * E)
                link(eng.tensor_scalar(wqk_h[:, :, cols], folded, scale, None, ALU.mult))
                eng.scalar_tensor_tensor(out=wqk_l[:, :, cols], in0=folded, scalar=scale, in1=wqk_h[:, :, cols].bitcast(fp32),
                                         op0=ALU.mult, op1=ALU.subtract).then_inc(s_wready, 1)
                eng.wait_ge(s_fold, 3)
                eng.tensor_scalar(qk_bias[:, op], p1[2][:, KE * op:KE * (op + 1)], scale, None, ALU.mult).then_inc(s_wready, 1)

            def edges(p, t):
                wait_read(eng, ("tok", p, 2 * t))
                wait_read(eng, ("tok", p, 2 * t + 1))
                h = hid[:, p, t].rearrange("p b e -> p (b e)")
                eng.tensor_tensor(h, h, absd[:, :], ALU.add).then_inc(s_edges, 1)

            def moments(src, st, m, done):
                for j in range(4):
                    ins = eng.bn_stats(st[:, j, :], src[:, j // 2, j % 2, :])
                link(ins)
                for j in range(4):
                    ins = eng.bn_aggr(m[:, j, :], st[:, j, :])
                ins.then_inc(done, 1)

            def tok_moments(p):
                eng.wait_ge(s_edges, NT * (p + 1))
                moments(hid[:, p], stats, mv, s_mv)

            def normalise(dst, src, m, r, done):
                for j in range(4):
                    ins = eng.tensor_scalar(dst[:, j // 2, j % 2, :], src[:, j // 2, j % 2, :], m[:, j, 0:1], r[:, j:j + 1],
                                            ALU.subtract, ALU.mult)
                ins.then_inc(done, 1)

            def tok_normalise(p):
                eng.wait_ge(s_rstd, p + 1)
                if p >= 1:
                    wait_filled(eng, ("xt", p - 1, KE - 1))
                normalise(xn, hid[:, p], mv, rstd, s_xn)

            def low_part(key, n_hi, dst, src_hi, bias=None):
                wait_filled(eng, key)
                eng.wait_ge(s_hi, n_hi)
                if bias is None:
                    ins = eng.tensor_tensor(dst, misc(key)[:, :], src_hi.bitcast(fp32), ALU.subtract)
                else:
                    ins = eng.scalar_tensor_tensor(out=dst, in0=misc(key)[:, :], scalar=bias, in1=src_hi.bitcast(fp32),
                                                   op0=ALU.add, op1=ALU.subtract)
                ins.then_inc(freed(key), 1)

            def xt_low(p, kf):
                low_part(("xt", p, kf), 6 * p + kf + 1, xt_l[:, kf], xt_h[:, kf])

            def qkv_out(p, i):
                key = ("qkv", p, i)
                if QKV[i] is None:
                    b = 2 * p + i // 3
                    wait_filled(eng, key)
                    if b >= 4:
                        eng.wait_ge(s_av, 4 * (b - 3))
                    for t in range(NT):
                        dst = vals[:, b % 4, t, 0:HEADS * VW].rearrange("p (h v) -> p h v", v=VW)[:, :, 0:D]
                        src = misc(key)[:, t * E:(t + 1) * E].rearrange("p (h d) -> p h d", d=D)
                        ins = eng.tensor_tensor(dst, src, bv2[:, t].rearrange("p (h d) -> p h d", d=D), ALU.add)
                        if t == 0:
                            link(ins)
                    ins.then_inc(freed(key), 1)
                else:
                    op, m = QKV[i]
                    n = 4 * p + op + 2 * m
                    low_part(key, 6 * p + 2 + op + 2 * m + 1, qk_l[:, n % 2], qk_h[:, n % 2], qk_bias[:, op, m:m + 1])

            def split_max(b, half):
                u = 2 * b + half
                eng.wait_ge(s_max, HEADS * b + 8 * (half + 1))
                if u >= 1:
                    wait_filled(eng, ("neg", (u - 1) // 2, (u - 1) % 2))
                src = negmax[:, :, half * 8:(half + 1) * 8]
                link(eng.tensor_copy(negsplit[:, :, 0].bitcast(fp32r), src))
                eng.tensor_tensor(negsplit[:, :, 1], src, negsplit[:, :, 0], ALU.subtract).then_inc(s_split, 1)

            def neg_rows(b, half):
                u = 2 * b + half
                key = ("neg", b, half)
                wait_filled(eng, key)
                if u >= 2:
                    eng.wait_ge(s_nst, 16 * (u - 1))
                eng.tensor_copy(negrow[:, u % 2], misc(key)[0:16, 0:N]).then_inc(freed(key), 1)

            def scale_out(b):
                for t in range(NT):
                    u = NT * b + t
                    key = ("out", b, t)
                    wait_filled(eng, key)
                    v = misc(key)[:, :].rearrange("p (h r) -> p h r", r=OROWS)
                    if b >= 1:
                        wait_read(eng, ("out", b - 1, t))
                    link(eng.reciprocal(recip[:, t], v[:, :, D]))
                    if u >= 2:
                        eng.wait_ge(s_h2, u - 1)
                    eng.tensor_tensor(att[:, u % 2, :].rearrange("p (h d) -> p h d", d=D), v[:, :, 0:D],
                                      recip[:, t].unsqueeze(2).broadcast_to([P, HEADS, D]), ALU.mult).then_inc(freed(key), 1)

            def ffn_norm(p):
                eng.wait_ge(s_h2, 2 * NT * (p + 1))
                moments(hid[:, p], stats, mv, s_mv2)
                eng.wait_ge(s_rs2, p + 1)
                if p >= 1:
                    eng.wait_ge(s_res, p)
                normalise(xp, hid[:, p], mv, rstd, s_xp)
                eng.wait_ge(s_xp, p + 1)
                moments(xp, stats3, mv3, s_mv3)
                eng.wait_ge(s_rs3, p + 1)
                if p >= 1:
                    wait_filled(eng, ("n3", p - 1, KE - 1))
                normalise(n3, xp, mv3, rstd3, s_n3)

            def nt_low(p):
                for kf in range(KE):
                    low_part(("n3", p, kf), 6 * PAIRS + KE * p + kf + 1, nt_l[:, kf], nt_h[:, kf])

            def y_low(p, f):
                n = FT * p + f
                eng.wait_ge(s_silu, n + 1)
                eng.tensor_tensor(y_l[:, p % 2, f], yf[:, n % 2], y_h[:, p % 2, f].bitcast(fp32), ALU.subtract).then_inc(s_y, 1)

            def add_residual(p, h):
                u = 2 * p + h
                eng.wait_ge(s_f2, 2 * (u + 1))
                eng.wait_ge(s_res, p + 1)
                if u >= 2:
                    eng.wait_ge(s_out[u % 2], 32 * (u // 2))
                eng.tensor_tensor(osb[:, u % 2], p2[u % 2][:, :], res[:, p % 2, 2 * h:2 * h + 2].rearrange("p j e -> p (j e)"),
                                  ALU.add).then_inc(s_osb, 1)

            for t in range(NT):
                edges(0, t)
            tok_moments(0)
            tok_normalise(0)
            for kf in range(KE):
                xt_low(0, kf)
            for i in range(6):
                qkv_out(0, i)
            gray_low(2)
            gray_low(3)
            for t in range(NT):
                edges(1, t)
            tok_moments(1)
            tok_normalise(1)
            for s in range(B + 2):
                if s >= 1 and s <= B:
                    split_max(s - 1, 1)
                for i in range(HEADS):
                    if s < B:
                        n = HEADS * s + i
                        eng.wait_ge(s_p1, n + 1)
                        eng.tensor_reduce(negmax[:, i % 2, i - i % 2:i - i % 2 + 2],
                                          p1[n % 3][:, :].rearrange("p (h k) -> p h k", h=2), AX.X, ALU.max, negate=True).then_inc(s_max, 1)
                    if 1 <= s <= B and i == AT_NEG1 + 1:
                        neg_rows(s - 1, 1)
                    if s >= 2 and i == AT_OUT + 1:
                        scale_out(s - 2)
                    if has_xt(s):
                        p = (s + 1) // 2
                        if i == AT_XT + 1:
                            for kf in range(KE):
                                xt_low(p, kf)
                        if i - 1 in AT_QKV:
                            qkv_out(p, AT_QKV.index(i - 1))
                    if has_tok(s):
                        p = s // 2 + 1
                        if i == 1:
                            gray_low(2 * p)
                            gray_low(2 * p + 1)
                        if i == AT_TOK[1] + 1:
                            edges(p, 0)
                        if i == AT_TOK[3] + 1:
                            edges(p, 1)
                            tok_moments(p)
                        if i == 14:
                            tok_normalise(p)
                    if s < B and i == 7:
                        split_max(s, 0)
                    if s < B and i == AT_NEG0 + 1:
                        neg_rows(s, 0)
                    if s == B - 1 and i in (5, 13):
                        eng.wait_ge(s_small, 16 * 7)
                        eng.wait_ge(s_w1f, 1)
                        k = i // 8
                        src, cols = wfull[:, k * F:(k + 1) * F], gamma[:, k:k + 1]
                        link(eng.tensor_scalar(w1_h[:, k], src, cols, None, ALU.mult))
                        eng.scalar_tensor_tensor(out=w1_l[:, k], in0=src, scalar=cols, in1=w1_h[:, k].bitcast(fp32),
                                                 op0=ALU.mult, op1=ALU.subtract).then_inc(s_w1r, 1)
                    if s == B and i == AT_OUT + 2:
                        ffn_norm(0)
                    if s == B and i == AT_N3 + 1:
                        nt_low(0)
                        eng.wait_ge(s_w1f, 2)
                        w2h, w2l = (w[:].rearrange("p f e -> p (f e)") for w in (w2_h, w2_l))
                        link(eng.tensor_copy(w2h, wfull[:]))
                        eng.tensor_tensor(w2l, wfull[:], w2h.bitcast(fp32), ALU.subtract).then_inc(s_w2r, 1)
                    if s == B - 1 and i == AT_B1 + 1:
                        key = ("b1", 0, 0)
                        wait_filled(eng, key)
                        eng.tensor_tensor(b1[:], misc(key)[:, 0:FT], b1col[:], ALU.add).then_inc(freed(key), 1)

            for p in range(PAIRS + 1):
                for f in range(FT):
                    if p < PAIRS:
                        y_low(p, f)
                    if p >= 1 and f in (3, 7):
                        add_residual(p - 1, f // 4)
                    if f == 1 and p + 1 < PAIRS:
                        ffn_norm(p + 1)
                if p + 1 < PAIRS:
                    nt_low(p + 1)

        @block.scalar
        def _(eng):
            eng.wait_ge(s_cleared, 1)
            for t in range(NT):
                row = P if t == 0 else P - 1
                for dx in range(3):
                    lo, hi = max(0, 1 - dx), E - max(0, dx - 1)
                    first = 3 * t + dx
                    eng.dma_start(halo_x[first:first + 6 * C - 5:6, :, lo:hi],
                                  x[:, :, row, lo + dx - 1:hi + dx - 1].rearrange("b c w -> c b w")).then_inc(s_halo, 16)
            for op in range(2):
                eng.wait_ge(s_wt, op + 1)
                eng.activation(wtr[:, op], p2[op][:, :], ACT.Copy).then_inc(s_wtc, 1)
            eng.wait_ge(s_halo, 16 * 3 * NT)
            for q in (0, 32):
                eng.activation(halo[q:q + 32], halo_x[:], ACT.Copy).then_inc(s_halo_h, 1)
            eng.wait_ge(s_zeros, 2)
            wide = zeros[:].unsqueeze(1).broadcast_to([P, HEADS, N])
            for b in range(2):
                eng.activation(ks[:, b], wide, ACT.Identity, bias=onecol[:]).then_inc(s_ones, 1)

            def edge(p, i):
                key = ("tok", p, i)
                t = i // 2
                wait_filled(eng, key)
                if i % 2 == 0:
                    if NT * p + t >= 1:
                        eng.wait_ge(s_edges, NT * p + t)
                    dst = absd[:]
                else:
                    dst = hid[:, p, t].rearrange("p b e -> p (b e)")
                eng.activation(dst, misc(key)[:, :], ACT.Abs).then_inc(freed(key), 1)

            def xt_high(p, kf):
                key = ("xt", p, kf)
                wait_filled(eng, key)
                if p >= 1:
                    wait_filled(eng, ("qkv", p - 1, 5))
                eng.activation(xt_h[:, kf], misc(key)[:, :], ACT.Copy).then_inc(s_hi, 1)

            def qk_high(p, i):
                if QKV[i] is None:
                    return
                op, m = QKV[i]
                n = 4 * p + op + 2 * m
                key = ("qkv", p, i)
                wait_filled(eng, key)
                if n >= 2:
                    eng.wait_ge(s_store[n % 2], 32 * (n // 2))
                eng.activation(qk_h[:, n % 2], misc(key)[:, :], ACT.Identity, bias=qk_bias[:, op, m:m + 1]).then_inc(s_hi, 1)

            def exp_head(b, i):
                n = HEADS * b + i
                eng.wait_ge(s_p2, n + 1)
                if n >= 8:
                    eng.wait_ge(s_av, (n - 8) // 4 + 1)
                eng.activation(probs[:, n % 8], p2[n % 2][:, :], ACT.Exp).then_inc(s_exp, 1)

            def copy_av(b, g):
                eng.wait_ge(s_av, 4 * b + g + 1)
                if g == 0 and b >= 1:
                    wait_filled(eng, ("out", b - 1, NT - 1))
                eng.activation(otr[:, g], av[:, 0:N], ACT.Copy).then_inc(s_ot, 1)

            def nt_high(p):
                for kf in range(KE):
                    key = ("n3", p, kf)
                    wait_filled(eng, key)
                    if p >= 1:
                        eng.wait_ge(s_f1, FT * p)
                    eng.activation(nt_h[:, kf], misc(key)[:, :], ACT.Copy).then_inc(s_hi, 1)

            for i in range(2 * NT):
                edge(0, i)
            for kf in range(KE):
                xt_high(0, kf)
            eng.wait_ge(s_wready, 5)
            for i in range(6):
                qk_high(0, i)
            for i in range(2 * NT):
                edge(1, i)
            for s in range(B + 2):
                for i in range(HEADS):
                    if 1 <= s <= B:
                        exp_head(s - 1, i)
                    if i == AT_AV_LAST and s >= 2:
                        copy_av(s - 2, 3)
                    if 1 <= s <= B and i in AT_AV:
                        copy_av(s - 1, AT_AV.index(i))
                    if has_xt(s) and i == AT_XT:
                        for kf in range(KE):
                            xt_high((s + 1) // 2, kf)
                    if has_xt(s) and i in AT_QKV:
                        qk_high((s + 1) // 2, AT_QKV.index(i))
                    if has_tok(s) and i in AT_TOK:
                        edge(s // 2 + 1, AT_TOK.index(i))
                    if s == B and i == AT_N3:
                        nt_high(0)

            wait_read(eng, ("b1", 0, 0))
            for p in range(PAIRS):
                for f in range(FT):
                    n = FT * p + f
                    src = p1[n % 3][:, :]
                    eng.wait_ge(s_f1, n + 1)
                    if p >= 2:
                        eng.wait_ge(s_f2, 4 * (p - 1))
                    eng.activation(y_h[:, p % 2, f], src, ACT.Silu, bias=b1[:, f:f + 1])
                    if n >= 2:
                        eng.wait_ge(s_y, n - 1)
                    eng.activation(yf[:, n % 2], src, ACT.Silu, bias=b1[:, f:f + 1]).then_inc(s_silu, 1)
                if p + 1 < PAIRS:
                    nt_high(p + 1)

        @block.tensor
        def _(eng):
            def product(dst, pairs, more_after=False):
                steps = [(l, r) for (lh, ll), (rh, rl) in pairs for l, r in ((lh, rh), (ll, rh), (lh, rl))]
                for i, (l, r) in enumerate(steps):
                    ins = eng.matmul(dst, l, r, start=i == 0, stop=i == len(steps) - 1 and not more_after)
                return ins

            def tok(p, i):
                t, k = i // 2, i % 2
                key = ("tok", p, i)
                wait_freed(eng, key)
                if i == 0:
                    eng.wait_ge(s_gray, 2 * (p + 1))
                dst = misc(key)[:, :].rearrange("p (b e) -> p b e", b=2)
                product(dst, [((band_h[:, k, dx], band_l[:, k, dx]),
                               (gray_h[:, t, :, dx:dx + E], gray_l[:, t, :, dx:dx + E])) for dx in range(3)], more_after=True)
                eng.matmul(dst, halo_b[:, t, k], halo[:, 2 * p:2 * p + 2, :], start=False, stop=True).then_inc(filled(key), 1)

            def xt(p, kf):
                key = ("xt", p, kf)
                wait_freed(eng, key)
                if kf == 0:
                    eng.wait_ge(s_xn, p + 1)
                for b in range(2):
                    for t in range(NT):
                        c = (NT * b + t) * P
                        ins = eng.transpose(misc(key)[:, c:c + P], xn[:, t, b, kf * P:(kf + 1) * P], ident[:])
                ins.then_inc(filled(key), 1)

            def qkv(p, i):
                key = ("qkv", p, i)
                wait_freed(eng, key)
                if i == 0:
                    for kf in range(KE):
                        wait_read(eng, ("xt", p, kf))
                if QKV[i] is None:
                    bb = i // 3
                    for t in range(NT):
                        c = (NT * bb + t) * P
                        ins = product(misc(key)[:, t * E:(t + 1) * E],
                                      [((xt_h[:, kf, c:c + P], xt_l[:, kf, c:c + P]), (wqk_h[:, kf, 2 * E:], wqk_l[:, kf, 2 * E:]))
                                       for kf in range(KE)])
                else:
                    op, m = QKV[i]
                    c = op * E + m * P
                    ins = product(misc(key)[:, :], [((wqk_h[:, kf, c:c + P], wqk_l[:, kf, c:c + P]), (xt_h[:, kf], xt_l[:, kf]))
                                                    for kf in range(KE)])
                ins.then_inc(filled(key), 1)

            def scores_by_query(b, i):
                n = HEADS * b + i
                if i % 8 == 0:
                    eng.wait_ge(s_load[b % 2][i // 8], 16 * 6 * (b // 2 + 1))
                if n >= 3:
                    eng.wait_ge(s_max, n - 2)
                t = i % 2
                for j in range(2):
                    h = i - t + j
                    ins = eng.matmul(p1[n % 3][:, j * N:(j + 1) * N], qs[0:MROW, b % 2, h, t * P:(t + 1) * P],
                                     ks[0:MROW, b % 2, h, :], start=True, stop=True)
                ins.then_inc(s_p1, 1)

            def scores_by_key(b, h):
                n = HEADS * b + h
                if h % 8 == 0:
                    eng.wait_ge(s_nld[h // 8], 16 * (b + 1))
                if n >= 2:
                    eng.wait_ge(s_exp, n - 1)
                for t in range(NT):
                    ins = eng.matmul(p2[n % 2][:, t * N:(t + 1) * N], ks[0:KSTACK, b % 2, h, t * P:(t + 1) * P],
                                     qs[0:KSTACK, b % 2, h, :], start=True, stop=True)
                ins.then_inc(s_p2, 1)

            def attend(b, g):
                n = 4 * b + g
                eng.wait_ge(s_exp, 4 * (n + 1))
                if g == 0:
                    key = ("qkv", b // 2, 2 + 3 * (b % 2))
                    wait_read(eng, key)
                if n >= 1:
                    eng.wait_ge(s_ot, n)
                for t in range(NT):
                    for j in range(4):
                        h = 4 * g + j
                        ins = eng.matmul(av[OROWS * j:OROWS * (j + 1), 0:N], vals[:, b % 4, t, h * VW:h * VW + OROWS],
                                         probs[:, (4 * n + j) % 8, t * N:(t + 1) * N], start=t == 0, stop=t == NT - 1)
                ins.then_inc(s_av, 1)

            def neg(b, half):
                key = ("neg", b, half)
                wait_freed(eng, key)
                eng.wait_ge(s_split, 2 * b + half + 1)
                for t in range(NT):
                    ins = eng.transpose(misc(key)[0:16, t * P:(t + 1) * P], negsplit[:, t].rearrange("p r h -> p (r h)"), ident[:])
                ins.then_inc(filled(key), 1)

            def out_rows(b):
                for t in range(NT):
                    key = ("out", b, t)
                    wait_freed(eng, key)
                    eng.wait_ge(s_ot, 4 * (b + 1))
                    for g in range(4):
                        ins = eng.transpose(misc(key)[:, g * P:(g + 1) * P], otr[:, g, t * P:(t + 1) * P], ident[:])
                    ins.then_inc(filled(key), 1)

            def n3_transposed(p):
                for kf in range(KE):
                    key = ("n3", p, kf)
                    wait_freed(eng, key)
                    eng.wait_ge(s_n3, p + 1)
                    for j in range(4):
                        ins = eng.transpose(misc(key)[:, j * P:(j + 1) * P], n3[:, j // 2, j % 2, kf * P:(kf + 1) * P], ident[:])
                    ins.then_inc(filled(key), 1)

            def fc1(p, f):
                n = FT * p + f
                if f == 0:
                    for k in range(KE):
                        wait_read(eng, ("n3", p, k))
                if n >= 3:
                    eng.wait_ge(s_silu, n - 2)
                product(p1[n % 3][:, :], [((w1_h[:, k, f * P:(f + 1) * P], w1_l[:, k, f * P:(f + 1) * P]), (nt_h[:, k], nt_l[:, k]))
                                                 for k in range(KE)]).then_inc(s_f1, 1)

            def fc2(p, j):
                u = 2 * p + j // 2
                if j == 0:
                    eng.wait_ge(s_y, FT * (p + 1))
                if u >= 2 and j % 2 == 0:
                    eng.wait_ge(s_osb, u - 1)
                rows = slice(j * P, (j + 1) * P)
                product(p2[u % 2][:, (j % 2) * E:(j % 2 + 1) * E],
                        [((y_h[:, p % 2, f, rows], y_l[:, p % 2, f, rows]), (w2_h[:, f], w2_l[:, f])) for f in range(FT)])\
                    .then_inc(s_f2, 1)

            eng.wait_ge(s_masks, 4)
            eng.wait_ge(s_wld, 16 * 5)
            for op in range(2):
                for m in range(KE):
                    for kf in range(KE):
                        c = (m * KE + kf) * P
                        ins = eng.transpose(p2[op][:, c:c + P], wsrc[:, op, kf, m * P:(m + 1) * P], ident[:])
                ins.then_inc(s_wt, 1)
            eng.wait_ge(s_masks, 5)
            for op in range(2):
                eng.wait_ge(s_wtc, op + 1)
                for kf in range(KE):
                    for m in range(KE):
                        c = (m * KE + kf) * P
                        ins = eng.matmul(p1[op][:, kf * E + m * P:kf * E + (m + 1) * P], wtr[:, op, c:c + P], wp_diag[:],
                                         start=True, stop=True)
                ins.then_inc(s_fold, 1)
            for op in range(2):
                for m in range(KE):
                    ins = eng.matmul(p1[2][:, KE * op + m:KE * op + m + 1], wp_diag[:], qk_bcol[:, op, m:m + 1], start=True, stop=True)
            ins.then_inc(s_fold, 1)

            eng.wait_ge(s_band, 1)
            eng.wait_ge(s_border, 4)
            eng.wait_ge(s_halo_w, 2)
            for i in range(2 * NT):
                tok(0, i)
            for kf in range(KE):
                xt(0, kf)
            eng.wait_ge(s_wready, 5)
            for i in range(6):
                qkv(0, i)
            for i in range(2 * NT):
                tok(1, i)
            for s in range(B + 2):
                for i in range(HEADS):
                    if s < B:
                        scores_by_query(s, i)
                    if 1 <= s <= B:
                        scores_by_key(s - 1, i)
                    if i == AT_AV_LAST and s >= 2:
                        attend(s - 2, 3)
                    if 1 <= s <= B and i in AT_AV:
                        attend(s - 1, AT_AV.index(i))
                    if i == AT_NEG1 and 1 <= s <= B:
                        neg(s - 1, 1)
                    if i == AT_OUT and s >= 2:
                        out_rows(s - 2)
                    if has_xt(s) and i == AT_XT:
                        for kf in range(KE):
                            xt((s + 1) // 2, kf)
                    if has_xt(s) and i in AT_QKV:
                        qkv((s + 1) // 2, AT_QKV.index(i))
                    if has_tok(s) and i in AT_TOK:
                        tok(s // 2 + 1, AT_TOK.index(i))
                    if i == AT_NEG0 and s < B:
                        neg(s, 0)
                    if s == B and i == AT_N3:
                        n3_transposed(0)
                    if s == B - 1 and i == AT_B1:
                        key = ("b1", 0, 0)
                        wait_freed(eng, key)
                        eng.wait_ge(s_w1f, 1)
                        eng.wait_ge(s_small, 16 * 7)
                        for f in range(FT):
                            for k in range(KE):
                                ins = eng.matmul(misc(key)[:, f:f + 1], wfull[:, k * F + f * P:k * F + (f + 1) * P], beta[:, k:k + 1],
                                                 start=k == 0, stop=k == KE - 1)
                        ins.then_inc(filled(key), 1)

            eng.wait_ge(s_w1r, 2)
            for f in range(FT):
                fc1(0, f)
            eng.wait_ge(s_w2r, 1)
            for p in range(PAIRS):
                if p + 1 < PAIRS:
                    n3_transposed(p + 1)
                for j in range(4):
                    for f in (2 * j, 2 * j + 1):
                        if p + 1 < PAIRS:
                            fc1(p + 1, f)
                    fc2(p, j)


_INS = ['x', 'L0_tok_scharr', 'L0_attn_Wq', 'L0_attn_bq', 'L0_attn_Wk', 'L0_attn_bk', 'L0_attn_Wv', 'L0_attn_bv', 'L0_attn_Wp',
        'L0_ffn_ln_gamma', 'L0_ffn_ln_beta', 'L0_ffn_fc1_q', 'L0_ffn_fc1_scales', 'L0_ffn_fc1_bias', 'L0_ffn_fc2_q',
        'L0_ffn_fc2_scales', 'L0_ffn_fc2_bias']


def kernel(**inputs):
    import numpy as _np
    import concourse.bacc as _bacc
    from concourse import mybir as _mybir
    from concourse.bass_utils import run_bass_kernel_spmd as _run

    nc = _bacc.Bacc("TRN2", target_bir_lowering=False, num_devices=1)
    arrays, args = {}, []
    for name in _INS:
        a = _np.ascontiguousarray(inputs[name])
        arrays[f"in_{name}"] = a
        args.append(nc.dram_tensor(f"in_{name}", a.shape, _mybir.dt.from_np(a.dtype), kind="ExternalInput").ap())
    args.append(nc.dram_tensor("out_0", (8, 256, 256), _mybir.dt.float32, kind="ExternalOutput").ap())
    vit_tower_kernel(nc, *args)
    r = _run(nc, [arrays], core_ids=[0])
    return r.results[0]["out_0"]
```

```python
import concourse.bass as bass
from concourse import mybir
from contextlib import ExitStack


def vit_tower_kernel(nc, x, scharr, Wq, bq, Wk, bk, Wv, bv, Wp, ln_gamma, ln_beta,
                     fc1_q, fc1_scales, fc1_bias, fc2_q, fc2_scales, fc2_bias, out):
    fp32 = mybir.dt.float32
    fp32r = mybir.dt.float32r
    i32 = mybir.dt.int32
    ALU = mybir.AluOpType
    ACT = mybir.ActivationFunctionType
    AX = mybir.AxisListType

    P = 128
    B, C, N, E = x.shape
    NT = N // P
    KE = E // P
    D = Wp.shape[0]
    HEADS = E // D
    HPT = P // D
    F = fc1_q.shape[1]
    FT = F // P
    PAIRS = B // 2
    COLS = 2 * N
    EPS = 1e-5
    GRAY = (0.2989, 0.587, 0.114)
    Q_SCALE = float(D) ** -0.5
    SPLIT = 3 * D
    MROW = 96
    KSTACK = MROW + 2
    VW = D + 1
    OROWS = 32

    KB = 1024
    base = (nc.sbuf_base + 63) // 64 * 64

    def at(name, kb, shape, dt):
        size = 4
        for n in shape[1:]:
            size *= n
        assert base + int(kb * KB) + size <= nc.sbuf_usable_end, name
        return nc.alloc_sbuf_tensor_at(name, shape, dt, offset=base + int(kb * KB))

    hid = at("hid", 0, [P, PAIRS, NT, 2, E], fp32)
    ident = at("ident", 16, [P, P], fp32)
    stats = at("stats", 16.5, [P, 4, 6], fp32)
    mv = at("mv", 16.625, [P, 4, 2], fp32)
    rstd = at("rstd", 16.75, [P, 4], fp32)
    mhalf = at("mhalf", 16.8125, [P, 4], fp32)
    vareps = at("vareps", 16.875, [P, 4], fp32)
    stats3 = at("stats3", 17, [P, 4, 6], fp32)
    mv3 = at("mv3", 17.125, [P, 4, 2], fp32)
    rstd3 = at("rstd3", 17.25, [P, 4], fp32)
    vareps3 = at("vareps3", 17.3125, [P, 4], fp32)
    negmax = at("negmax", 17.375, [P, NT, HEADS], fp32)
    qk_bias = at("qk_bias", 17.5, [P, 2, KE], fp32)
    qk_bcol = at("qk_bcol", 17.5625, [P, 2, KE], fp32)
    recip = at("recip", 24.75, [P, 2, HEADS], fp32)
    gamma = at("gamma", 17.6875, [P, KE], fp32)
    beta = at("beta", 17.75, [P, KE], fp32)
    b1col = at("b1col", 17.8125, [P, FT], fp32)
    b1 = at("b1", 17.875, [P, FT], fp32)
    halo_m = at("halo_m", 17.9375, [P, NT, 3], fp32)
    halo_p = at("halo_p", 18, [P, NT, 2, 3], fp32)
    halo_w = at("halo_w", 18.0625, [P, NT * 2], fp32)
    halo_wh = at("halo_wh", 18.125, [P, NT * 2], fp32r)
    halo_wl = at("halo_wl", 18.1875, [P, NT * 2], fp32)
    s_all = at("s_all", 18.25, [P, 18], fp32)
    onecol = at("onecol", 18.375, [P, 1], fp32)
    unused = at("unused", 18.4375, [P, 1], fp32)
    negsplit = at("negsplit", 18.5, [P, NT, 2, 8], fp32)
    negrow = at("negrow", 18.75, [16, 2, N], fp32r)
    b2 = at("b2", 20.75, [P, 4, E], fp32)

    xr = at("xr", 25, [P, 2, C, NT, E], fp32)
    gray = at("gray", 37, [P, 2, NT, E], fp32)
    gray_h = at("gray_h", 41, [P, NT, 2, E + 2], fp32r)
    gray_l = at("gray_l", 45.25, [P, NT, 2, E + 2], fp32r)
    band_h = at("band_h", 49.5, [P, 2, 3, P], fp32r)
    band_l = at("band_l", 52.5, [P, 2, 3, P], fp32r)
    halo = at("halo", 55.5, [P, B, E], fp32r)
    halo_b = at("halo_b", 63.5, [P, NT, 2, P], fp32r)
    w1_h = at("w1_h", 25, [P, KE, F], fp32r)
    w1_l = at("w1_l", 33, [P, KE, F], fp32r)
    wraw = at("wraw", 41, [P, KE * F], i32)
    wscale = at("wscale", 49, [P, KE * F], fp32)
    wfull = at("wfull", 57, [P, KE * F], fp32)

    xn = at("xn", 66, [P, NT, 2, E], fp32)
    xt_h = at("xt_h", 70, [P, KE, COLS], fp32r)
    xt_l = at("xt_l", 74, [P, KE, COLS], fp32r)
    qk_h = at("qk_h", 78, [P, 2, COLS], fp32r)
    qk_l = at("qk_l", 82, [P, 2, COLS], fp32r)
    wqk_h = at("wqk_h", 86, [P, KE, 3 * E], fp32r)
    wqk_l = at("wqk_l", 92, [P, KE, 3 * E], fp32r)
    bv2 = at("bv2", 98, [P, NT, E], fp32)
    vals = at("vals", 100, [P, 4, NT, HEADS * VW + 16], fp32)
    otr = at("otr", 109.25, [P, 4, N], fp32)
    absd = at("absd", 113.25, [P, COLS], fp32)
    att = at("att", 115.25, [P, 2, E], fp32)
    probs = at("probs", 117.25, [P, 8, NT * N], fp32)
    qs = at("qs", 133.25, [P, 2, HEADS, N], fp32r)
    ks = at("ks", 165.25, [P, 2, HEADS, N], fp32r)
    assert 197.25 + 8 <= (nc.sbuf_usable_end - base) / KB
    zeros = at("zeros", 205.25, [P, E], fp32)
    masks = at("masks", 117.25, [P, 3, P], fp32)
    band = at("band", 119, [P, 2, 3, P], fp32)
    halo_x = at("halo_x", 122.25, [32, B, E], fp32)
    wsrc = at("wsrc", 197.25, [P, 2, KE, E], fp32)
    wtr = at("wtr", 201.25, [P, 2, KE * E], fp32)
    wv_src = at("wv_src", 109.25, [P, KE, E], fp32)
    wp_diag = at("wp_diag", 111.25, [P, P], fp32)
    wp_rep = at("wp_rep", 111.75, [P, D], fp32)

    w2_h = at("w2_h", 66, [P, FT, E], fp32r)
    w2_l = at("w2_l", 74, [P, FT, E], fp32r)
    nt_h = [at("nt_h0", 82, [P, KE, COLS], fp32r), at("nt_h1", 41, [P, KE, COLS], fp32r)]
    nt_l = [at("nt_l0", 86, [P, KE, COLS], fp32r), at("nt_l1", 45, [P, KE, COLS], fp32r)]
    xp = [at("xp0", 90, [P, NT, 2, E], fp32), at("xp1", 197.25, [P, NT, 2, E], fp32)]
    n3 = [at("n30", 94, [P, NT, 2, E], fp32), at("n31", 201.25, [P, NT, 2, E], fp32)]
    res = at("res", 98, [P, 2, 4, E], fp32)
    yf = at("yf", 117.25, [P, 2, COLS], fp32)
    osb = at("osb", 121.25, [P, 2, COLS], fp32)
    y_h = at("y_h", 133.25, [P, 2, FT, COLS], fp32r)
    y_l = at("y_l", 165.25, [P, 2, FT, COLS], fp32r)

    qk_dram = nc.dram_tensor("qk_parts", [PAIRS, 2, 2, E, COLS], fp32).ap()

    ctx = ExitStack()
    with ctx:
        def bank(name):
            return ctx.enter_context(nc.psum_tensor(name, [P, COLS], fp32))

        def sem(name):
            return ctx.enter_context(nc.semaphore(name))

        p1 = [bank("p1a"), bank("p1b"), bank("p1c")]
        p2 = [bank("p2a"), bank("p2b")]
        av = bank("av")
        mi = [bank("mia"), bank("mib")]

        s_scharr = sem("scharr_loaded")
        s_cleared = sem("cleared")
        s_halo = sem("halo_loaded")
        s_wsrc = sem("wq_wk_loaded")
        s_wld = sem("wv_loaded")
        s_wpd = sem("wp_loaded")
        s_x = [sem("x_loaded0"), sem("x_loaded1")]
        s_wraw = sem("ffn_weights_loaded")
        s_small = sem("small_loaded")
        s_masks = sem("masks_ready")
        s_ident = sem("identity_ready")
        s_diag = sem("wp_diagonal_ready")
        s_zero = sem("zeroed")
        s_zeros = sem("zeros_ready")
        s_border = sem("gray_borders_zeroed")
        s_ones = sem("stacks_preset")
        s_band = sem("band_ready")
        s_halo_h = sem("halo_high_ready")
        s_halo_w = sem("halo_operands_ready")
        s_wt = sem("w_transposed")
        s_wtc = sem("w_transpose_copied")
        s_fold = sem("w_folded")
        s_wready = sem("qkv_weights_ready")
        s_dv = sem("vector_chain")
        s_pl = sem("pool_chain")
        s_gray = sem("gray_split")
        s_grayp = [sem("gray_ready0"), sem("gray_ready1")]
        s_grayh = [sem("gray_high_ready0"), sem("gray_high_ready1")]
        s_edges = sem("edges_added")
        s_mv = sem("moments_ready")
        s_rstd = sem("rstd_ready")
        s_xn = sem("xn_ready")
        s_fill = [sem("misc_filled0"), sem("misc_filled1")]
        s_free = [sem("misc_freed0"), sem("misc_freed1")]
        s_hi = sem("high_part_ready")
        s_store = [sem("qk_stored0"), sem("qk_stored1")]
        s_load = [[sem(f"qk_loaded{b}{h}") for h in range(2)] for b in range(2)]
        s_p1 = sem("p1_scores")
        s_max = sem("maxima")
        s_split = sem("neg_max_split")
        s_nld = [sem("neg_rows_loaded0"), sem("neg_rows_loaded1")]
        s_p2 = sem("p2_scores")
        s_exp = sem("exps")
        s_av = sem("av_groups")
        s_ot = sem("av_copied")
        s_h2 = sem("attention_added")
        s_w1f = sem("w_full")
        s_w1r = sem("w1_ready")
        s_w2r = sem("w2_ready")
        s_mv2 = sem("moments2")
        s_rs2 = sem("rstd2")
        s_xp = sem("xp_ready")
        s_mv3 = sem("moments3")
        s_rs3 = sem("rstd3_ready")
        s_n3 = sem("n3_ready")
        s_res = sem("residual_ready")
        s_f1 = sem("fc1_done")
        s_silu = sem("silu_done")
        s_y = sem("y_ready")
        s_f2 = sem("fc2_done")
        s_osb = sem("out_rows_ready")
        s_out = [sem("out_stored0"), sem("out_stored1")]

        turns = []

        def tok_turns(p):
            turns.extend(("tok", p, i) for i in range(2 * NT))

        def xt_turns(p):
            turns.extend(("xt", p, i) for i in range(KE))

        def qkv_turns(p):
            turns.extend(("qkv", p, i) for i in range(6))

        QKV = [(0, 0), (1, 0), None, (0, 1), (1, 1), None]
        tok_turns(0)
        xt_turns(0)
        qkv_turns(0)
        turns.extend([("tok", 1, 0), ("tok", 1, 1)])
        AT_AV = (7, 11, 15)
        AT_AV_LAST, AT_OUT = 2, (3, 4)
        AT_NEG0, AT_NEG1 = 9, 2
        AT_TOK, AT_TOK1 = (5, 7, 10, 12), (2, 6)
        AT_XT, AT_QKV = (5, 6), (8, 9, 11, 12, 13, 14)
        AT_NORM = (6, 9, 11, 14)
        AT_B1, AT_N3, AT_FC1 = 12, 7, (10, 12, 14)

        def has_xt(s):
            return s % 2 == 1 and (s + 1) // 2 < PAIRS

        def has_tok(s):
            return s % 2 == 0 and s >= 2 and s // 2 + 1 < PAIRS

        for s in range(B + 2):
            for i in range(HEADS):
                if i == AT_NEG1 and 1 <= s <= B:
                    turns.append(("neg", s - 1, 1))
                if i in AT_OUT and s >= 2:
                    turns.append(("out", s - 2, AT_OUT.index(i)))
                if has_xt(s) and i in AT_XT:
                    turns.append(("xt", (s + 1) // 2, AT_XT.index(i)))
                if has_xt(s) and i in AT_QKV:
                    turns.append(("qkv", (s + 1) // 2, AT_QKV.index(i)))
                if has_tok(s) and i in AT_TOK:
                    turns.append(("tok", s // 2 + 1, AT_TOK.index(i)))
                if s == 0 and i in AT_TOK1:
                    turns.append(("tok", 1, 2 + AT_TOK1.index(i)))
                if i == AT_NEG0 and s < B:
                    turns.append(("neg", s, 0))
                if s == B - 1 and i == AT_B1:
                    turns.append(("b1", 0, 0))
                if s == B and i == AT_N3:
                    turns.extend(("n3", 0, kf) for kf in range(KE))
        for p in range(1, PAIRS):
            turns.extend(("n3", p, kf) for kf in range(KE))
        turn = {key: n for n, key in enumerate(turns)}
        assert len(turn) == len(turns)

        def misc(key):
            return mi[turn[key] % 2]

        def wait_filled(eng, key):
            n = turn[key]
            eng.wait_ge(s_fill[n % 2], n // 2 + 1)

        def wait_freed(eng, key):
            n = turn[key]
            if n >= 2:
                eng.wait_ge(s_free[n % 2], n // 2)

        def wait_read(eng, key):
            n = turn[key]
            eng.wait_ge(s_free[n % 2], n // 2 + 1)

        def filled(key):
            return s_fill[turn[key] % 2]

        def freed(key):
            return s_free[turn[key] % 2]

        block = ctx.enter_context(nc.Block())

        @block.sync
        def _(eng):
            def load_x(b):
                if b >= 2:
                    eng.wait_ge(s_grayp[b % 2], b // 2)
                eng.dma_start(xr[:, b % 2], x[b].rearrange("c (t p) w -> p c t w", p=P)).then_inc(s_x[b % 2], 16)

            def store_qk(p, i):
                n = 4 * p + i
                op, m = (i % 2, i // 2)
                wait_read(eng, ("qkv", p, i + i // 2))
                for part, src in enumerate((qk_h, qk_l)):
                    eng.dma_start(qk_dram[p, op, part, m * P:(m + 1) * P, :], src[:, n % 2, :].bitcast(fp32)).then_inc(s_store[n % 2], 16)

            def load_qk(b, half):
                p = b // 2
                for r in range(2):
                    eng.wait_ge(s_store[r], 32 * (2 * p + half + 1))
                if b >= 2:
                    eng.wait_ge(s_p2, HEADS * (b - 2) + 8 * (half + 1))
                else:
                    eng.wait_ge(s_ones, 4)
                cols = slice((b % 2) * N, (b % 2 + 1) * N)
                for dst, op, parts in ((qs, 0, (0, 1, 0)), (ks, 1, (0, 0, 1))):
                    for slot, part in enumerate(parts):
                        src = qk_dram[p, op, part, half * P:(half + 1) * P, cols].rearrange("(h d) t -> d h t", d=D)
                        eng.dma_start(dst[slot * D:(slot + 1) * D, b % 2, half * HPT:(half + 1) * HPT, :].bitcast(fp32), src)\
                           .then_inc(s_load[b % 2][half], 16)

            def pass_neg(b, half):
                u = 2 * b + half
                wait_read(eng, ("neg", b, half))
                if b >= 2:
                    eng.wait_ge(s_p2, HEADS * (b - 2) + 8 * (half + 1))
                for part in range(2):
                    eng.dma_start(qs[MROW + part:MROW + part + 1, b % 2, half * HPT:(half + 1) * HPT, :].bitcast(fp32),
                                  negrow[part * HPT:(part + 1) * HPT, u % 2, :].bitcast(fp32)).then_inc(s_nld[half], 16)

            def load_ffn(layer, part):
                q, sc, tiles = ((fc1_q, fc1_scales, KE), (fc2_q, fc2_scales, FT))[layer]
                lo, hi = (part % 2) * tiles // 2, (part % 2 + 1) * tiles // 2
                n = KE * F // tiles
                if part < 2:
                    dst, src = wraw, q.rearrange("(k p) n -> p k n", p=P)[:, lo:hi]
                    eng.dma_start(dst[:, lo * n:hi * n].rearrange("p (k n) -> p k n", k=hi - lo), src).then_inc(s_wraw, 16)
                else:
                    src = sc[lo:hi].rearrange("(a g) n -> a (g n)", a=1).broadcast_to([P, (hi - lo) * n])
                    eng.dma_start(wscale[:, lo * n:hi * n], src).then_inc(s_wraw, 16)

            eng.dma_start(s_all[:], scharr.rearrange("k o a b -> o (k a b)").broadcast_to([P, 18])).then_inc(s_scharr, 16)
            load_x(0)
            eng.dma_start(wsrc[:, 0], Wq.rearrange("(k p) n -> p k n", p=P)).then_inc(s_wsrc, 16)
            eng.dma_start(wsrc[:, 1], Wk.rearrange("(k p) n -> p k n", p=P)).then_inc(s_wsrc, 16)
            eng.dma_start(wp_rep[:], Wp.unsqueeze(0).broadcast_to([HPT, D, D])).then_inc(s_wpd, 16)
            load_x(1)
            for i, src in enumerate((bq, bk)):
                eng.dma_start(qk_bcol[:, i, :], src.rearrange("(m p) -> p m", p=P), allow_slow_non_contiguous=True).then_inc(s_wpd, 16)
            eng.dma_start(wv_src[:], Wv.rearrange("(k p) n -> p k n", p=P)).then_inc(s_wld, 16)
            for t in range(NT):
                eng.dma_start(bv2[:, t, :], bv.rearrange("(a n) -> a n", a=1).broadcast_to([P, E])).then_inc(s_wld, 16)
            load_x(2)
            load_x(3)
            for dst, src in ((gamma, ln_gamma), (beta, ln_beta), (b1col, fc1_bias)):
                eng.dma_start(dst[:], src.rearrange("(m p) -> p m", p=P), allow_slow_non_contiguous=True).then_inc(s_small, 16)
            for j in range(4):
                eng.dma_start(b2[:, j, :], fc2_bias.rearrange("(a n) -> a n", a=1).broadcast_to([P, E])).then_inc(s_small, 16)
            for i in range(4):
                store_qk(0, i)
            for half in range(2):
                load_qk(0, half)
            for half in range(2):
                load_qk(1, half)
            load_x(4)
            load_x(5)
            for s in range(B + 1):
                if s >= 1:
                    pass_neg(s - 1, 1)
                if s == 2:
                    load_x(6)
                    load_x(7)
                if s == 5:
                    load_ffn(0, 1)
                    load_ffn(0, 2)
                if s == 7:
                    eng.wait_ge(s_w1f, 1)
                    load_ffn(1, 0)
                    load_ffn(1, 1)
                if has_xt(s):
                    store_qk((s + 1) // 2, 0)
                    store_qk((s + 1) // 2, 1)
                if s < B:
                    pass_neg(s, 0)
                if s == 5:
                    load_ffn(0, 3)
                if 1 <= s and s + 1 < B:
                    load_qk(s + 1, 0)
                if has_xt(s):
                    store_qk((s + 1) // 2, 2)
                    store_qk((s + 1) // 2, 3)
                if 1 <= s and s + 1 < B:
                    load_qk(s + 1, 1)
                if s == 4:
                    wait_filled(eng, ("tok", PAIRS - 1, 2 * NT - 1))
                    load_ffn(0, 0)
                if s == 7:
                    load_ffn(1, 2)
                    load_ffn(1, 3)
            for p in range(PAIRS):
                for h in range(2):
                    u = 2 * p + h
                    eng.wait_ge(s_osb, u + 1)
                    for b in range(2):
                        dst = out[2 * p + b, h * P:(h + 1) * P, :]
                        eng.dma_start(dst, osb[:, u % 2, b * E:(b + 1) * E]).then_inc(s_out[u % 2], 16)
            for r in range(2):
                eng.wait_ge(s_out[r], 32 * PAIRS)

        @block.gpsimd
        def _(eng):
            chain = [0]

            def link(ins):
                chain[0] += 1
                ins.then_inc(s_pl, 1)
                eng.wait_ge(s_pl, chain[0])

            eng.memset(ident[:], 0.0).then_inc(s_zero, 1)
            eng.wait_ge(s_zero, 1)
            eng.affine_select(out=ident[:], in_=ident[:], compare_op=ALU.not_equal, fill=1.0,
                              base=0, pattern=[[-1, P]], channel_multiplier=1).then_inc(s_ident, 1)
            eng.wait_ge(s_ident, 1)
            eng.memset(halo_x[:], 0.0).then_inc(s_cleared, 1)
            link(eng.memset(masks[:], 0.0))
            for r in range(3):
                ins = eng.affine_select(out=masks[:, r], in_=masks[:, r], compare_op=ALU.not_equal, fill=1.0,
                                        base=1 - r, pattern=[[-1, P]], channel_multiplier=1)
                ins.then_inc(s_masks, 1)
            link(eng.memset(onecol[:], 0.0))
            eng.memset(zeros[:], 0.0).then_inc(s_zeros, 1)
            eng.wait_ge(s_zeros, 1)
            eng.memset(onecol[MROW:P], 1.0).then_inc(s_zeros, 1)
            eng.wait_ge(s_zeros, 2)
            link(eng.memset(halo_m[:], 0.0))
            for q in (0, 32, 64):
                for c in range(C):
                    rows = halo_m[q:q + 32]
                    link(eng.affine_select(out=rows, in_=rows, compare_op=ALU.not_equal, fill=GRAY[c],
                                           base=-6 * c, pattern=[[-3, NT], [-1, 3]], channel_multiplier=1))
            eng.memset(halo[96:128].bitcast(fp32), 0.0).then_inc(s_zero, 1)
            eng.wait_ge(s_zero, 2)
            eng.wait_ge(s_wpd, 48)
            diag = wp_diag[:].rearrange("p (h e) -> p h e", e=D)
            link(eng.affine_select(out=diag, in_=wp_rep[:].unsqueeze(1).broadcast_to([P, HPT, D]), compare_op=ALU.is_ge, fill=0.0,
                                   base=0, pattern=[[-D, HPT], [0, D]], channel_multiplier=1))
            eng.affine_select(out=diag, in_=diag, compare_op=ALU.is_ge, fill=0.0,
                              base=D - 1, pattern=[[D, HPT], [0, D]], channel_multiplier=-1).then_inc(s_diag, 1)
            eng.wait_ge(s_diag, 1)
            eng.memset(mhalf[:], -0.5).then_inc(s_zero, 1)
            def rstd_of(mv_t, ve, dst, ready, n, done, js=slice(0, 4)):
                eng.wait_ge(ready, n)
                link(eng.tensor_scalar(ve[:, js], mv_t[:, js, 1], EPS, 1.0, ALU.add, ALU.mult))
                eng.tensor_tensor(dst[:, js], ve[:, js], mhalf[:, js], ALU.pow).then_inc(done, 1)

            def tok_rstd(p, t):
                rstd_of(mv, vareps, rstd, s_mv, NT * p + t + 1, s_rstd, slice(2 * t, 2 * t + 2))

            def gray_image(b):
                p = b // 2
                eng.wait_ge(s_x[b % 2], 16 * (b // 2 + 1))
                g = gray[:, b % 2]
                if b >= 2:
                    eng.wait_ge(s_gray, b - 1)
                ch = [xr[:, b % 2, c] for c in range(C)]
                link(eng.tensor_scalar(g, ch[0], GRAY[0], 0.0, ALU.mult, ALU.add))
                for c in range(1, C):
                    link(eng.tensor_scalar(ch[c], ch[c], GRAY[c], 0.0, ALU.mult, ALU.add))
                    ins = eng.tensor_tensor(g, g, ch[c], ALU.add)
                    if c < C - 1:
                        link(ins)
                ins.then_inc(s_grayp[b % 2], 1)
                eng.wait_ge(s_grayp[b % 2], b // 2 + 1)
                if p >= 1:
                    wait_filled(eng, ("tok", p - 1, 2 * NT - 1))
                eng.tensor_scalar(gray_h[:, :, b % 2, 1:E + 1], g, 1.0, 0.0, ALU.mult, ALU.add).then_inc(s_grayh[b % 2], 1)

            def add_attention(b):
                for t in range(NT):
                    u = NT * b + t
                    wait_read(eng, ("out", b, t))
                    h = hid[:, b // 2, t, b % 2, :]
                    eng.tensor_tensor(h, h, att[:, u % 2, :], ALU.add).then_inc(s_h2, 1)

            gray_image(1)
            eng.memset(vals[:], 1.0).then_inc(s_zero, 1)
            for t in range(NT):
                tok_rstd(0, t)
            gray_image(2)
            gray_image(3)
            for b in range(2):
                eng.memset(qs[:, b].bitcast(fp32), 0.0).then_inc(s_ones, 1)
            for t in range(NT):
                tok_rstd(1, t)
            for s in range(1, B + 2):
                if s == B:
                    eng.wait_ge(s_wraw, 128)
                    eng.wait_ge(s_w1r, 2)
                    wait_filled(eng, ("b1", 0, 0))
                    link(eng.tensor_scalar(wfull[:], wraw[:], -128.0, 0.5, ALU.add, ALU.mult))
                    eng.tensor_tensor(wfull[:], wfull[:], wscale[:], ALU.mult).then_inc(s_w1f, 1)
                if s >= 2:
                    add_attention(s - 2)
                if s in (B - 2, B):
                    q = s // B
                    rstd_of(mv, vareps, rstd, s_mv2, q + 1, s_rs2)
                    rstd_of(mv3, vareps3, rstd3, s_mv3, q + 1, s_rs3)
                if s in (1, 3):
                    gray_image(s + 3)
                    gray_image(s + 4)
                if s in (2, 4):
                    for t in range(NT):
                        tok_rstd(s // 2 + 1, t)
                if s == 6:
                    eng.wait_ge(s_wraw, 64)
                    link(eng.tensor_scalar(wfull[:], wraw[:], -128.0, 1.0, ALU.add, ALU.mult))
                    eng.tensor_tensor(wfull[:], wfull[:], wscale[:], ALU.mult).then_inc(s_w1f, 1)
            eng.wait_ge(s_small, 16 * 7)
            link(eng.tensor_scalar(b2[:], b2[:], 0.5, 0.0, ALU.mult, ALU.add))
            for p in range(PAIRS):
                eng.wait_ge(s_xp, p + 1)
                if p >= 2:
                    eng.wait_ge(s_osb, 2 * (p - 1))
                r = res[:, p % 2].rearrange("p j e -> p (j e)")
                link(eng.tensor_tensor(r, hid[:, p].rearrange("p t b e -> p (t b e)"), xp[p % 2][:].rearrange("p t b e -> p (t b e)"), ALU.add))
                eng.tensor_tensor(r, r, b2[:].rearrange("p j e -> p (j e)"), ALU.add).then_inc(s_res, 1)
                if p + 2 < PAIRS:
                    rstd_of(mv, vareps, rstd, s_mv2, p + 3, s_rs2)
                    rstd_of(mv3, vareps3, rstd3, s_mv3, p + 3, s_rs3)

        @block.vector
        def _(eng):
            chain = [0]

            def link(ins):
                chain[0] += 1
                ins.then_inc(s_dv, 1)
                eng.wait_ge(s_dv, chain[0])

            for g in (gray_h, gray_l):
                for c in (0, E + 1):
                    eng.memset(g[:, :, :, c:c + 1].bitcast(fp32), 0.0).then_inc(s_border, 1)
            eng.wait_ge(s_scharr, 16)
            eng.wait_ge(s_masks, 3)
            for dy in range(3):
                for k in range(2):
                    for dx in range(3):
                        w = s_all[:, 9 * k + 3 * dy + dx:9 * k + 3 * dy + dx + 1]
                        if dy == 0:
                            ins = eng.tensor_scalar(band[:, k, dx], masks[:, dy], w, None, ALU.mult)
                        else:
                            ins = eng.scalar_tensor_tensor(out=band[:, k, dx], in0=masks[:, dy], scalar=w,
                                                           in1=band[:, k, dx], op0=ALU.mult, op1=ALU.add)
                link(ins)
            link(eng.tensor_scalar(band_h[:], band[:], 0.5, None, ALU.mult))
            eng.scalar_tensor_tensor(out=band_l[:].rearrange("p k d j -> p (k d j)"), in0=band[:].rearrange("p k d j -> p (k d j)"),
                                     scalar=0.5, in1=band_h[:].rearrange("p k d j -> p (k d j)").bitcast(fp32),
                                     op0=ALU.mult, op1=ALU.subtract).then_inc(s_band, 1)

            def gray_first(b):
                eng.wait_ge(s_x[b % 2], 16)
                g = gray[:, b % 2]
                link(eng.tensor_scalar(g, xr[:, b % 2, 0], GRAY[0], None, ALU.mult))
                link(eng.scalar_tensor_tensor(out=g, in0=xr[:, b % 2, 1], scalar=GRAY[1], in1=g, op0=ALU.mult, op1=ALU.add))
                eng.scalar_tensor_tensor(out=g, in0=xr[:, b % 2, 2], scalar=GRAY[2], in1=g, op0=ALU.mult, op1=ALU.add).then_inc(s_grayp[b % 2], 1)
                eng.wait_ge(s_grayp[b % 2], b // 2 + 1)
                eng.tensor_scalar(gray_h[:, :, b % 2, 1:E + 1], g, 1.0, None, ALU.mult).then_inc(s_grayh[b % 2], 1)

            def gray_low(b):
                eng.wait_ge(s_grayh[b % 2], b // 2 + 1)
                eng.tensor_tensor(gray_l[:, :, b % 2, 1:E + 1], gray[:, b % 2], gray_h[:, :, b % 2, 1:E + 1].bitcast(fp32),
                                  ALU.subtract).then_inc(s_gray, 1)

            gray_first(0)
            gray_low(0)
            eng.wait_ge(s_zero, 2)
            for t in range(NT):
                dy = 2 if t == 0 else 0
                ins = eng.tensor_tensor(halo_p[:, t], halo_m[:, t].unsqueeze(1).broadcast_to([P, 2, 3]),
                                        s_all[:].rearrange("p (k a) -> p k a", k=2)[:, :, 3 * dy:3 * dy + 3], ALU.mult)
            link(ins)
            link(eng.tensor_reduce(halo_w[:], halo_p[:].rearrange("p t k x -> p (t k) x"), AX.X, ALU.add))
            link(eng.tensor_scalar(halo_wh[:], halo_w[:], 0.5, None, ALU.mult))
            link(eng.scalar_tensor_tensor(out=halo_wl[:], in0=halo_w[:], scalar=0.5, in1=halo_wh[:].bitcast(fp32),
                                          op0=ALU.mult, op1=ALU.subtract))
            eng.wait_ge(s_halo_h, 2)
            eng.tensor_tensor(halo[64:96], halo_x[:], halo[0:32].bitcast(fp32), ALU.subtract).then_inc(s_halo_w, 1)
            gray_low(1)
            link(eng.memset(halo_b[:].bitcast(fp32), 0.0))
            for t in range(NT):
                edge = P - 1 if t == 0 else 0
                link(eng.tensor_copy(halo_b[:, t, :, edge], halo_wh[:, 2 * t:2 * t + 2].bitcast(fp32)))
                ins = eng.tensor_copy(halo_b[32:64, t, :, edge], halo_wl[32:64, 2 * t:2 * t + 2])
                if t == 0:
                    link(ins)
            ins.then_inc(s_halo_w, 1)

            eng.wait_ge(s_wld, 16 * (NT + 1))
            link(eng.tensor_copy(wqk_h[:, :, 2 * E:], wv_src[:]))
            eng.tensor_tensor(wqk_l[:, :, 2 * E:], wv_src[:], wqk_h[:, :, 2 * E:].bitcast(fp32), ALU.subtract).then_inc(s_wready, 1)
            for op in range(2):
                scale = Q_SCALE if op == 0 else 1.0
                eng.wait_ge(s_fold, op + 1)
                folded = p1[op][:, :].rearrange("p (k n) -> p k n", k=KE)
                cols = slice(op * E, (op + 1) * E)
                link(eng.tensor_scalar(wqk_h[:, :, cols], folded, scale, None, ALU.mult))
                eng.scalar_tensor_tensor(out=wqk_l[:, :, cols], in0=folded, scalar=scale, in1=wqk_h[:, :, cols].bitcast(fp32),
                                         op0=ALU.mult, op1=ALU.subtract).then_inc(s_wready, 1)
                eng.wait_ge(s_fold, 3)
                eng.tensor_scalar(qk_bias[:, op], p1[2][:, KE * op:KE * (op + 1)], scale, None, ALU.mult).then_inc(s_wready, 1)

            def edges(p, t):
                wait_read(eng, ("tok", p, 2 * t))
                wait_read(eng, ("tok", p, 2 * t + 1))
                h = hid[:, p, t].rearrange("p b e -> p (b e)")
                eng.tensor_tensor(h, h, absd[:, :], ALU.add).then_inc(s_edges, 1)

            def moments(src, st, m, done, js=range(4)):
                for j in js:
                    ins = eng.bn_stats(st[:, j, :], src[:, j // 2, j % 2, :])
                link(ins)
                for j in js:
                    ins = eng.bn_aggr(m[:, j, :], st[:, j, :])
                ins.then_inc(done, 1)

            def tok_moments(p, t):
                eng.wait_ge(s_edges, NT * p + t + 1)
                moments(hid[:, p], stats, mv, s_mv, (2 * t, 2 * t + 1))

            def normalise(dst, src, m, r, done, js=range(4)):
                for j in js:
                    ins = eng.tensor_scalar(dst[:, j // 2, j % 2, :], src[:, j // 2, j % 2, :], m[:, j, 0:1], r[:, j:j + 1],
                                            ALU.subtract, ALU.mult)
                ins.then_inc(done, 1)

            def tok_normalise(p, t):
                eng.wait_ge(s_rstd, NT * p + t + 1)
                if p >= 1 and t == 0:
                    wait_filled(eng, ("xt", p - 1, KE - 1))
                normalise(xn, hid[:, p], mv, rstd, s_xn, (2 * t, 2 * t + 1))

            def low_part(key, n_hi, dst, src_hi, bias=None):
                wait_filled(eng, key)
                eng.wait_ge(s_hi, n_hi)
                if bias is None:
                    ins = eng.tensor_tensor(dst, misc(key)[:, :], src_hi.bitcast(fp32), ALU.subtract)
                else:
                    ins = eng.scalar_tensor_tensor(out=dst, in0=misc(key)[:, :], scalar=bias, in1=src_hi.bitcast(fp32),
                                                   op0=ALU.add, op1=ALU.subtract)
                ins.then_inc(freed(key), 1)

            def xt_low(p, kf):
                low_part(("xt", p, kf), 6 * p + kf + 1, xt_l[:, kf], xt_h[:, kf])

            def qkv_out(p, i):
                key = ("qkv", p, i)
                if QKV[i] is None:
                    b = 2 * p + i // 3
                    wait_filled(eng, key)
                    if b >= 4:
                        eng.wait_ge(s_av, 4 * (b - 3))
                    for t in range(NT):
                        dst = vals[:, b % 4, t, 0:HEADS * VW].rearrange("p (h v) -> p h v", v=VW)[:, :, 0:D]
                        src = misc(key)[:, t * E:(t + 1) * E].rearrange("p (h d) -> p h d", d=D)
                        ins = eng.tensor_tensor(dst, src, bv2[:, t].rearrange("p (h d) -> p h d", d=D), ALU.add)
                        if t == 0:
                            link(ins)
                    ins.then_inc(freed(key), 1)
                else:
                    op, m = QKV[i]
                    n = 4 * p + op + 2 * m
                    low_part(key, 6 * p + 2 + op + 2 * m + 1, qk_l[:, n % 2], qk_h[:, n % 2], qk_bias[:, op, m:m + 1])

            def split_max(b, half):
                u = 2 * b + half
                eng.wait_ge(s_max, HEADS * b + 8 * (half + 1))
                if u >= 1:
                    wait_filled(eng, ("neg", (u - 1) // 2, (u - 1) % 2))
                src = negmax[:, :, half * 8:(half + 1) * 8]
                link(eng.tensor_copy(negsplit[:, :, 0].bitcast(fp32r), src))
                eng.tensor_tensor(negsplit[:, :, 1], src, negsplit[:, :, 0], ALU.subtract).then_inc(s_split, 1)

            def neg_rows(b, half):
                u = 2 * b + half
                key = ("neg", b, half)
                wait_filled(eng, key)
                if u >= 2:
                    eng.wait_ge(s_nld[half], 32 * b)
                eng.tensor_copy(negrow[:, u % 2], misc(key)[0:16, 0:N]).then_inc(freed(key), 1)

            def scale_out(b, t):
                u = NT * b + t
                key = ("out", b, t)
                wait_filled(eng, key)
                v = misc(key)[:, :].rearrange("p (h r) -> p h r", r=OROWS)
                if b >= 1:
                    wait_read(eng, ("out", b - 1, t))
                link(eng.reciprocal(recip[:, t], v[:, :, D]))
                if u >= 2:
                    eng.wait_ge(s_h2, u - 1)
                eng.tensor_tensor(att[:, u % 2, :].rearrange("p (h d) -> p h d", d=D), v[:, :, 0:D],
                                  recip[:, t].unsqueeze(2).broadcast_to([P, HEADS, D]), ALU.mult).then_inc(freed(key), 1)

            def ffn_norm(p, part):
                if part == 0:
                    eng.wait_ge(s_h2, 2 * NT * (p + 1))
                    moments(hid[:, p], stats, mv, s_mv2)
                elif part == 1:
                    eng.wait_ge(s_rs2, p + 1)
                    if p >= 2:
                        eng.wait_ge(s_res, p - 1)
                    normalise(xp[p % 2], hid[:, p], mv, rstd, s_xp)
                elif part == 2:
                    eng.wait_ge(s_xp, p + 1)
                    moments(xp[p % 2], stats3, mv3, s_mv3)
                else:
                    eng.wait_ge(s_rs3, p + 1)
                    if p >= 2:
                        wait_filled(eng, ("n3", p - 2, KE - 1))
                    normalise(n3[p % 2], xp[p % 2], mv3, rstd3, s_n3)

            def nt_low(p):
                for kf in range(KE):
                    low_part(("n3", p, kf), 6 * PAIRS + KE * p + kf + 1, nt_l[p % 2][:, kf], nt_h[p % 2][:, kf])

            def y_low(p, f):
                n = FT * p + f
                eng.wait_ge(s_silu, n + 1)
                eng.tensor_tensor(y_l[:, p % 2, f], yf[:, n % 2], y_h[:, p % 2, f].bitcast(fp32), ALU.subtract).then_inc(s_y, 1)

            def add_residual(p, h):
                u = 2 * p + h
                eng.wait_ge(s_f2, 2 * (u + 1))
                eng.wait_ge(s_res, p + 1)
                if u >= 2:
                    eng.wait_ge(s_out[u % 2], 32 * (u // 2))
                eng.tensor_tensor(osb[:, u % 2], p2[u % 2][:, :], res[:, p % 2, 2 * h:2 * h + 2].rearrange("p j e -> p (j e)"),
                                  ALU.add).then_inc(s_osb, 1)

            for t in range(NT):
                edges(0, t)
                tok_moments(0, t)
                tok_normalise(0, t)
            for kf in range(KE):
                xt_low(0, kf)
            for i in range(6):
                qkv_out(0, i)
                if i in (1, 3):
                    gray_low(2 + i // 2)
            edges(1, 0)
            for s in range(B + 2):
                if s >= 1 and s <= B:
                    split_max(s - 1, 1)
                for i in range(HEADS):
                    if s < B:
                        n = HEADS * s + i
                        eng.wait_ge(s_p1, n + 1)
                        eng.tensor_reduce(negmax[:, i % 2, i - i % 2:i - i % 2 + 2],
                                          p1[n % 3][:, :].rearrange("p (h k) -> p h k", h=2), AX.X, ALU.max, negate=True).then_inc(s_max, 1)
                    if 1 <= s <= B and i == AT_NEG1 + 1:
                        neg_rows(s - 1, 1)
                    if s >= 2 and i - 1 in AT_OUT:
                        scale_out(s - 2, AT_OUT.index(i - 1))
                    if has_xt(s):
                        p = (s + 1) // 2
                        if s == 1 and i < NT:
                            tok_moments(p, i)
                        if s == 1 and NT <= i < 2 * NT:
                            tok_normalise(p, i - NT)
                        if i - 1 in AT_XT:
                            xt_low(p, AT_XT.index(i - 1))
                        if i - 1 in AT_QKV:
                            qkv_out(p, AT_QKV.index(i - 1))
                    if s == 0 and i == AT_TOK1[1] + 1:
                        edges(1, 1)
                    if has_tok(s):
                        p = s // 2 + 1
                        if i == 1:
                            gray_low(2 * p)
                            gray_low(2 * p + 1)
                        if i == AT_TOK[1] + 1:
                            edges(p, 0)
                        if i == AT_TOK[3] + 1:
                            edges(p, 1)
                            for t in range(NT):
                                tok_moments(p, t)
                        if i == 15:
                            for t in range(NT):
                                tok_normalise(p, t)
                    if s < B and i == 7:
                        split_max(s, 0)
                    if s < B and i == AT_NEG0 + 1:
                        neg_rows(s, 0)
                    if s == B - 1 and i in (5, 13):
                        eng.wait_ge(s_small, 16 * 7)
                        eng.wait_ge(s_w1f, 1)
                        k = i // 8
                        src, cols = wfull[:, k * F:(k + 1) * F], gamma[:, k:k + 1]
                        link(eng.tensor_scalar(w1_h[:, k], src, cols, None, ALU.mult))
                        eng.scalar_tensor_tensor(out=w1_l[:, k], in0=src, scalar=cols, in1=w1_h[:, k].bitcast(fp32),
                                                 op0=ALU.mult, op1=ALU.subtract).then_inc(s_w1r, 1)
                    if s in (B - 2, B) and i in AT_NORM:
                        ffn_norm(s // B, AT_NORM.index(i))
                    if s == B and i == AT_N3 + 1:
                        nt_low(0)
                    if s == B and i == 15:
                        eng.wait_ge(s_w1f, 2)
                        w2h, w2l = (w[:].rearrange("p f e -> p (f e)") for w in (w2_h, w2_l))
                        link(eng.tensor_copy(w2h, wfull[:]))
                        eng.tensor_tensor(w2l, wfull[:], w2h.bitcast(fp32), ALU.subtract).then_inc(s_w2r, 1)
                    if s == B - 1 and i == AT_B1 + 1:
                        key = ("b1", 0, 0)
                        wait_filled(eng, key)
                        eng.tensor_tensor(b1[:], misc(key)[:, 0:FT], b1col[:], ALU.add).then_inc(freed(key), 1)

            for p in range(PAIRS + 1):
                for f in range(FT):
                    if p < PAIRS:
                        y_low(p, f)
                    if p >= 1 and f in (3, 7):
                        add_residual(p - 1, f // 4)
                    if f == 3 and p + 1 < PAIRS:
                        nt_low(p + 1)
                    if f >= 4 and p + 2 < PAIRS:
                        ffn_norm(p + 2, f - 4)

        @block.scalar
        def _(eng):
            eng.wait_ge(s_cleared, 1)
            for t in range(NT):
                row = P if t == 0 else P - 1
                for dx in range(3):
                    lo, hi = max(0, 1 - dx), E - max(0, dx - 1)
                    first = 3 * t + dx
                    eng.dma_start(halo_x[first:first + 6 * C - 5:6, :, lo:hi],
                                  x[:, :, row, lo + dx - 1:hi + dx - 1].rearrange("b c w -> c b w")).then_inc(s_halo, 16)
            for op in range(2):
                eng.wait_ge(s_wt, op + 1)
                eng.activation(wtr[:, op], p2[op][:, :], ACT.Copy).then_inc(s_wtc, 1)
            eng.wait_ge(s_halo, 16 * 3 * NT)
            for q in (0, 32):
                eng.activation(halo[q:q + 32], halo_x[:], ACT.Copy).then_inc(s_halo_h, 1)
            eng.wait_ge(s_zeros, 2)
            wide = zeros[:].unsqueeze(1).broadcast_to([P, HEADS, N])
            for b in range(2):
                eng.activation(ks[:, b], wide, ACT.Identity, bias=onecol[:]).then_inc(s_ones, 1)

            def edge(p, i):
                key = ("tok", p, i)
                t = i // 2
                wait_filled(eng, key)
                if i % 2 == 0:
                    if NT * p + t >= 1:
                        eng.wait_ge(s_edges, NT * p + t)
                    dst = absd[:]
                else:
                    dst = hid[:, p, t].rearrange("p b e -> p (b e)")
                eng.activation(dst, misc(key)[:, :], ACT.Abs).then_inc(freed(key), 1)

            def xt_high(p, kf):
                key = ("xt", p, kf)
                wait_filled(eng, key)
                if p >= 1:
                    wait_filled(eng, ("qkv", p - 1, 5))
                eng.activation(xt_h[:, kf], misc(key)[:, :], ACT.Copy).then_inc(s_hi, 1)

            def qk_high(p, i):
                if QKV[i] is None:
                    return
                op, m = QKV[i]
                n = 4 * p + op + 2 * m
                key = ("qkv", p, i)
                wait_filled(eng, key)
                if n >= 2:
                    eng.wait_ge(s_store[n % 2], 32 * (n // 2))
                eng.activation(qk_h[:, n % 2], misc(key)[:, :], ACT.Identity, bias=qk_bias[:, op, m:m + 1]).then_inc(s_hi, 1)

            def exp_head(b, i):
                n = HEADS * b + i
                eng.wait_ge(s_p2, n + 1)
                if n >= 8:
                    eng.wait_ge(s_av, (n - 8) // 4 + 1)
                eng.activation(probs[:, n % 8], p2[n % 2][:, :], ACT.Exp).then_inc(s_exp, 1)

            def copy_av(b, g):
                eng.wait_ge(s_av, 4 * b + g + 1)
                if g == 0 and b >= 1:
                    wait_filled(eng, ("out", b - 1, NT - 1))
                eng.activation(otr[:, g], av[:, 0:N], ACT.Copy).then_inc(s_ot, 1)

            def nt_high(p):
                for kf in range(KE):
                    key = ("n3", p, kf)
                    wait_filled(eng, key)
                    if p >= 2:
                        eng.wait_ge(s_f1, FT * (p - 1))
                    eng.activation(nt_h[p % 2][:, kf], misc(key)[:, :], ACT.Copy).then_inc(s_hi, 1)

            for i in range(2 * NT):
                edge(0, i)
            for kf in range(KE):
                xt_high(0, kf)
            eng.wait_ge(s_wready, 5)
            for i in range(6):
                qk_high(0, i)
            for i in range(2):
                edge(1, i)
            for s in range(B + 2):
                for i in range(HEADS):
                    if 1 <= s <= B:
                        exp_head(s - 1, i)
                    if i == AT_AV_LAST and s >= 2:
                        copy_av(s - 2, 3)
                    if 1 <= s <= B and i in AT_AV:
                        copy_av(s - 1, AT_AV.index(i))
                    if has_xt(s) and i in AT_XT:
                        xt_high((s + 1) // 2, AT_XT.index(i))
                    if has_xt(s) and i in AT_QKV:
                        qk_high((s + 1) // 2, AT_QKV.index(i))
                    if s == 0 and i in AT_TOK1:
                        edge(1, 2 + AT_TOK1.index(i))
                    if has_tok(s) and i in AT_TOK:
                        edge(s // 2 + 1, AT_TOK.index(i))
                    if s == B and i == AT_N3:
                        nt_high(0)

            eng.activation(unused[:], onecol[:], ACT.Silu)
            wait_read(eng, ("b1", 0, 0))
            for p in range(PAIRS):
                for f in range(FT):
                    n = FT * p + f
                    src = p1[n % 3][:, :]
                    eng.wait_ge(s_f1, n + 1)
                    if p >= 2:
                        eng.wait_ge(s_f2, 4 * (p - 1))
                    eng.activation(y_h[:, p % 2, f], src, ACT.Silu, bias=b1[:, f:f + 1])
                    if n >= 2:
                        eng.wait_ge(s_y, n - 1)
                    eng.activation(yf[:, n % 2], src, ACT.Silu, bias=b1[:, f:f + 1]).then_inc(s_silu, 1)
                    if f == 3 and p + 1 < PAIRS:
                        nt_high(p + 1)

        @block.tensor
        def _(eng):
            def product(dst, pairs, more_after=False):
                steps = [(l, r) for (lh, ll), (rh, rl) in pairs for l, r in ((lh, rh), (ll, rh), (lh, rl))]
                for i, (l, r) in enumerate(steps):
                    ins = eng.matmul(dst, l, r, start=i == 0, stop=i == len(steps) - 1 and not more_after)
                return ins

            def tok(p, i):
                t, k = i // 2, i % 2
                key = ("tok", p, i)
                wait_freed(eng, key)
                if i == 0:
                    eng.wait_ge(s_gray, 2 * (p + 1))
                dst = misc(key)[:, :].rearrange("p (b e) -> p b e", b=2)
                product(dst, [((band_h[:, k, dx], band_l[:, k, dx]),
                               (gray_h[:, t, :, dx:dx + E], gray_l[:, t, :, dx:dx + E])) for dx in range(3)], more_after=True)
                eng.matmul(dst, halo_b[:, t, k], halo[:, 2 * p:2 * p + 2, :], start=False, stop=True).then_inc(filled(key), 1)

            def xt(p, kf):
                key = ("xt", p, kf)
                wait_freed(eng, key)
                if kf == 0:
                    eng.wait_ge(s_xn, NT * (p + 1))
                for b in range(2):
                    for t in range(NT):
                        c = (NT * b + t) * P
                        ins = eng.transpose(misc(key)[:, c:c + P], xn[:, t, b, kf * P:(kf + 1) * P], ident[:])
                ins.then_inc(filled(key), 1)

            def qkv(p, i):
                key = ("qkv", p, i)
                wait_freed(eng, key)
                if i == 0:
                    for kf in range(KE):
                        wait_read(eng, ("xt", p, kf))
                if QKV[i] is None:
                    bb = i // 3
                    for t in range(NT):
                        c = (NT * bb + t) * P
                        ins = product(misc(key)[:, t * E:(t + 1) * E],
                                      [((xt_h[:, kf, c:c + P], xt_l[:, kf, c:c + P]), (wqk_h[:, kf, 2 * E:], wqk_l[:, kf, 2 * E:]))
                                       for kf in range(KE)])
                else:
                    op, m = QKV[i]
                    c = op * E + m * P
                    ins = product(misc(key)[:, :], [((wqk_h[:, kf, c:c + P], wqk_l[:, kf, c:c + P]), (xt_h[:, kf], xt_l[:, kf]))
                                                    for kf in range(KE)])
                ins.then_inc(filled(key), 1)

            def scores_by_query(b, i):
                n = HEADS * b + i
                if i % 8 == 0:
                    eng.wait_ge(s_load[b % 2][i // 8], 16 * 6 * (b // 2 + 1))
                if n >= 3:
                    eng.wait_ge(s_max, n - 2)
                t = i % 2
                for j in range(2):
                    h = i - t + j
                    ins = eng.matmul(p1[n % 3][:, j * N:(j + 1) * N], qs[0:MROW, b % 2, h, t * P:(t + 1) * P],
                                     ks[0:MROW, b % 2, h, :], start=True, stop=True)
                ins.then_inc(s_p1, 1)

            def scores_by_key(b, h):
                n = HEADS * b + h
                if h % 8 == 0:
                    eng.wait_ge(s_nld[h // 8], 32 * (b + 1))
                if n >= 2:
                    eng.wait_ge(s_exp, n - 1)
                for t in range(NT):
                    ins = eng.matmul(p2[n % 2][:, t * N:(t + 1) * N], ks[0:KSTACK, b % 2, h, t * P:(t + 1) * P],
                                     qs[0:KSTACK, b % 2, h, :], start=True, stop=True)
                ins.then_inc(s_p2, 1)

            def attend(b, g):
                n = 4 * b + g
                eng.wait_ge(s_exp, 4 * (n + 1))
                if g == 0:
                    key = ("qkv", b // 2, 2 + 3 * (b % 2))
                    wait_read(eng, key)
                if n >= 1:
                    eng.wait_ge(s_ot, n)
                for t in range(NT):
                    for j in range(4):
                        h = 4 * g + j
                        ins = eng.matmul(av[OROWS * j:OROWS * (j + 1), 0:N], vals[:, b % 4, t, h * VW:h * VW + OROWS],
                                         probs[:, (4 * n + j) % 8, t * N:(t + 1) * N], start=t == 0, stop=t == NT - 1)
                ins.then_inc(s_av, 1)

            def neg(b, half):
                key = ("neg", b, half)
                wait_freed(eng, key)
                eng.wait_ge(s_split, 2 * b + half + 1)
                for t in range(NT):
                    ins = eng.transpose(misc(key)[0:16, t * P:(t + 1) * P], negsplit[:, t].rearrange("p r h -> p (r h)"), ident[:])
                ins.then_inc(filled(key), 1)

            def out_rows(b, t):
                key = ("out", b, t)
                wait_freed(eng, key)
                eng.wait_ge(s_ot, 4 * (b + 1))
                for g in range(4):
                    ins = eng.transpose(misc(key)[:, g * P:(g + 1) * P], otr[:, g, t * P:(t + 1) * P], ident[:])
                ins.then_inc(filled(key), 1)

            def n3_transposed(p):
                for kf in range(KE):
                    key = ("n3", p, kf)
                    wait_freed(eng, key)
                    eng.wait_ge(s_n3, p + 1)
                    for j in range(4):
                        ins = eng.transpose(misc(key)[:, j * P:(j + 1) * P], n3[p % 2][:, j // 2, j % 2, kf * P:(kf + 1) * P], ident[:])
                    ins.then_inc(filled(key), 1)

            def fc2(p, j):
                u = 2 * p + j // 2
                if j == 0:
                    eng.wait_ge(s_y, FT * (p + 1))
                if u >= 2 and j % 2 == 0:
                    eng.wait_ge(s_osb, u - 1)
                rows = slice(j * P, (j + 1) * P)
                product(p2[u % 2][:, (j % 2) * E:(j % 2 + 1) * E],
                        [((y_h[:, p % 2, f, rows], y_l[:, p % 2, f, rows]), (w2_h[:, f], w2_l[:, f])) for f in range(FT)])\
                    .then_inc(s_f2, 1)

            def fc1(p, f):
                n = FT * p + f
                if f == 0:
                    for k in range(KE):
                        wait_read(eng, ("n3", p, k))
                if n >= 3:
                    eng.wait_ge(s_silu, n - 2)
                product(p1[n % 3][:, :], [((w1_h[:, k, f * P:(f + 1) * P], w1_l[:, k, f * P:(f + 1) * P]), (nt_h[p % 2][:, k], nt_l[p % 2][:, k]))
                                                 for k in range(KE)]).then_inc(s_f1, 1)

            eng.wait_ge(s_ident, 1)
            eng.wait_ge(s_wsrc, 32)
            for op in range(2):
                for m in range(KE):
                    for kf in range(KE):
                        c = (m * KE + kf) * P
                        ins = eng.transpose(p2[op][:, c:c + P], wsrc[:, op, kf, m * P:(m + 1) * P], ident[:])
                ins.then_inc(s_wt, 1)
            eng.wait_ge(s_diag, 1)
            for op in range(2):
                eng.wait_ge(s_wtc, op + 1)
                for kf in range(KE):
                    for m in range(KE):
                        c = (m * KE + kf) * P
                        ins = eng.matmul(p1[op][:, kf * E + m * P:kf * E + (m + 1) * P], wtr[:, op, c:c + P], wp_diag[:],
                                         start=True, stop=True)
                ins.then_inc(s_fold, 1)
            for op in range(2):
                for m in range(KE):
                    ins = eng.matmul(p1[2][:, KE * op + m:KE * op + m + 1], wp_diag[:], qk_bcol[:, op, m:m + 1], start=True, stop=True)
            ins.then_inc(s_fold, 1)

            eng.wait_ge(s_band, 1)
            eng.wait_ge(s_border, 4)
            eng.wait_ge(s_halo_w, 2)
            for i in range(2 * NT):
                tok(0, i)
            for kf in range(KE):
                xt(0, kf)
            eng.wait_ge(s_wready, 5)
            for i in range(6):
                qkv(0, i)
            for i in range(2):
                tok(1, i)
            for s in range(B + 2):
                for i in range(HEADS):
                    if s < B:
                        scores_by_query(s, i)
                    if 1 <= s <= B:
                        scores_by_key(s - 1, i)
                    if i == AT_AV_LAST and s >= 2:
                        attend(s - 2, 3)
                    if 1 <= s <= B and i in AT_AV:
                        attend(s - 1, AT_AV.index(i))
                    if i == AT_NEG1 and 1 <= s <= B:
                        neg(s - 1, 1)
                    if i in AT_OUT and s >= 2:
                        out_rows(s - 2, AT_OUT.index(i))
                    if has_xt(s) and i in AT_XT:
                        xt((s + 1) // 2, AT_XT.index(i))
                    if has_xt(s) and i in AT_QKV:
                        qkv((s + 1) // 2, AT_QKV.index(i))
                    if s == 0 and i in AT_TOK1:
                        tok(1, 2 + AT_TOK1.index(i))
                    if has_tok(s) and i in AT_TOK:
                        tok(s // 2 + 1, AT_TOK.index(i))
                    if i == AT_NEG0 and s < B:
                        neg(s, 0)
                    if s == B and i == AT_N3:
                        n3_transposed(0)
                    if s == B and i in AT_FC1:
                        if i == AT_FC1[0]:
                            eng.wait_ge(s_w1r, 2)
                        fc1(0, AT_FC1.index(i))
                    if s == B - 1 and i == AT_B1:
                        key = ("b1", 0, 0)
                        wait_freed(eng, key)
                        eng.wait_ge(s_w1f, 1)
                        eng.wait_ge(s_small, 16 * 7)
                        for f in range(FT):
                            for k in range(KE):
                                ins = eng.matmul(misc(key)[:, f:f + 1], wfull[:, k * F + f * P:k * F + (f + 1) * P], beta[:, k:k + 1],
                                                 start=k == 0, stop=k == KE - 1)
                        ins.then_inc(filled(key), 1)

            for f in range(len(AT_FC1), FT):
                if f == FT // 2:
                    n3_transposed(1)
                fc1(0, f)
            eng.wait_ge(s_w2r, 1)
            for p in range(PAIRS):
                for j in range(4):
                    if j == 2 and p + 2 < PAIRS:
                        n3_transposed(p + 2)
                    for f in (2 * j, 2 * j + 1):
                        if p + 1 < PAIRS:
                            fc1(p + 1, f)
                    fc2(p, j)


_INS = ['x', 'L0_tok_scharr', 'L0_attn_Wq', 'L0_attn_bq', 'L0_attn_Wk', 'L0_attn_bk', 'L0_attn_Wv', 'L0_attn_bv', 'L0_attn_Wp',
        'L0_ffn_ln_gamma', 'L0_ffn_ln_beta', 'L0_ffn_fc1_q', 'L0_ffn_fc1_scales', 'L0_ffn_fc1_bias', 'L0_ffn_fc2_q',
        'L0_ffn_fc2_scales', 'L0_ffn_fc2_bias']


def kernel(**inputs):
    import numpy as _np
    import concourse.bacc as _bacc
    from concourse import mybir as _mybir
    from concourse.bass_utils import run_bass_kernel_spmd as _run

    nc = _bacc.Bacc("TRN2", target_bir_lowering=False, num_devices=1)
    arrays, args = {}, []
    for name in _INS:
        a = _np.ascontiguousarray(inputs[name])
        arrays[f"in_{name}"] = a
        args.append(nc.dram_tensor(f"in_{name}", a.shape, _mybir.dt.from_np(a.dtype), kind="ExternalInput").ap())
    args.append(nc.dram_tensor("out_0", (8, 256, 256), _mybir.dt.float32, kind="ExternalOutput").ap())
    vit_tower_kernel(nc, *args)
    r = _run(nc, [arrays], core_ids=[0])
    return r.results[0]["out_0"]
```
